# Optimizing a Trainium2 kernel written in Bass

```python
import numpy as np
import jax
import jax.numpy as jnp

def _softmax(x, axis=-1):
    return jax.nn.softmax(x, axis=axis)

def _gelu(x):
    return jax.nn.gelu(x, approximate=True)

def _silu(x):
    return jax.nn.silu(x)

def _sigmoid(x):
    return jax.nn.sigmoid(x)

def _layernorm(x, axis=-1, eps=1e-05):
    m = jnp.mean(x, axis=axis, keepdims=True)
    v = jnp.var(x, axis=axis, keepdims=True)
    return (x - m) / jnp.sqrt(v + eps)

def _scatter_add(tgt, idx, src, axis=0):
    return tgt.at[idx].add(src)

def _segment_sum(src, seg, n):
    return jax.ops.segment_sum(src, seg, n)
kernel_name = 'mk_gnn_resnorm_d2_gnn_r8_87a663'

def setup_inputs(seed: int=0):
    np.random.seed(seed)
    _w = jnp.asarray

    def _rec_inputs():
        import jax
        import jax.numpy as jnp
        _gk = jax.random.key(seed)
        x = -0.0005121 + 1.001 * jax.random.normal(jax.random.fold_in(_gk, 1), (12500, 64), jnp.float32)
        src = jax.random.randint(jax.random.fold_in(_gk, 2), (200000,), 0, 12500, jnp.int32)
        dst = jnp.minimum((12500 * jax.random.uniform(jax.random.fold_in(_gk, 3), (200000,)) ** 2.0).astype(jnp.int32), 99999)
        _o = jnp.argsort(dst, stable=True)
        src = src[_o]
        dst = dst[_o]
        edge_attr_16 = 0.000196303 + 1.00016 * jax.random.normal(jax.random.fold_in(_gk, 11), (200000, 16), jnp.float32)
        return (x, src, dst, edge_attr_16)
    x, src, dst, edge_attr_16 = _rec_inputs()

    def _L0_gnn_setup():
        import jax, jax.numpy as jnp
        import numpy as np
        N = 6250
        E = 100000
        C = 64

        def _linear_params(key, fan_in, fan_out):
            kw, kb = jax.random.split(key)
            s = 1.0 / np.sqrt(fan_in)
            W = jax.random.uniform(kw, (fan_in, fan_out), jnp.float32, -s, s)
            b = jax.random.uniform(kb, (fan_out,), jnp.float32, -s, s)
            return (W, b)

        def _cgconv(x, edge_index, Wf, bf, Ws, bs):
            j, i = (edge_index[0], edge_index[1])
            z = jnp.concatenate([x[i], x[j]], axis=-1)
            m = jax.nn.sigmoid(z @ Wf + bf) * jax.nn.softplus(z @ Ws + bs)
            agg = jax.ops.segment_sum(m, i, num_segments=x.shape[0])
            return x + agg
        key = jax.random.key(seed)
        ks = jax.random.split(key, 6)
        x = jax.random.normal(ks[0], (N, C), jnp.float32)
        edge_index = jax.random.randint(ks[1], (2, E), 0, N, dtype=jnp.int64)
        Wf1, bf1 = _linear_params(ks[2], 2 * C, C)
        Ws1, bs1 = _linear_params(ks[3], 2 * C, C)
        Wf2, bf2 = _linear_params(ks[4], 2 * C, C)
        Ws2, bs2 = _linear_params(ks[5], 2 * C, C)
        return {'x': x, 'edge_index': edge_index, 'Wf1': Wf1, 'bf1': bf1, 'Ws1': Ws1, 'bs1': bs1, 'Wf2': Wf2, 'bf2': bf2, 'Ws2': Ws2, 'bs2': bs2}
    _L0_gnn_all = _L0_gnn_setup()
    _L0_gnn_in = {k: v for k, v in _L0_gnn_all.items() if k in ('Wf1', 'bf1', 'Ws1', 'bs1', 'Wf2', 'bf2', 'Ws2', 'bs2')}
    del _L0_gnn_all

    def _L1_gnn_setup():
        import jax, jax.numpy as jnp
        import numpy as np
        N = 12500
        E = 200000
        IN_D = 64
        H_D = 64
        OUT_D = 64
        EDGE_D = 16
        HEADS = 1
        NEG_SLOPE = 0.2
        BN_EPS = 1e-05

        def gat_conv(x, src, dst, edge_attr, W, We, att_s, att_d, att_e, bias):
            n = x.shape[0]
            C = W.shape[1] // HEADS
            deg = jax.ops.segment_sum(jnp.ones((src.shape[0],), x.dtype), dst, num_segments=n)
            loop_attr = jax.ops.segment_sum(edge_attr, dst, num_segments=n) / jnp.clip(deg, 1.0)[:, None]
            src2 = jnp.concatenate([src, jnp.arange(n, dtype=src.dtype)])
            dst2 = jnp.concatenate([dst, jnp.arange(n, dtype=dst.dtype)])
            ea2 = jnp.concatenate([edge_attr, loop_attr], axis=0)
            xl = (x @ W).reshape(n, HEADS, C)
            a_src = (xl * att_s).sum(-1)
            a_dst = (xl * att_d).sum(-1)
            el = (ea2 @ We).reshape(-1, HEADS, C)
            a_edge = (el * att_e).sum(-1)
            alpha = a_src[src2] + a_dst[dst2] + a_edge
            alpha = jax.nn.leaky_relu(alpha, NEG_SLOPE)
            amax = jax.ops.segment_max(alpha, dst2, num_segments=n)
            ex = jnp.exp(alpha - amax[dst2])
            den = jax.ops.segment_sum(ex, dst2, num_segments=n)
            p = ex / den[dst2]
            out = jax.ops.segment_sum(xl[src2] * p[..., None], dst2, num_segments=n)
            return out.mean(axis=1) + bias

        def batch_norm(h, gamma, beta):
            m = h.mean(axis=0)
            v = h.var(axis=0)
            return gamma * (h - m) * jax.lax.rsqrt(v + BN_EPS) + beta
        key = jax.random.key(seed)
        ks = jax.random.split(key, 24)

        def nrm(k, shape, scale=1.0):
            return jax.random.normal(k, shape, dtype=jnp.float32) * scale
        inp = {'x': nrm(ks[0], (N, IN_D)), 'edge_index': jax.random.randint(ks[1], (2, E), 0, N, dtype=jnp.int64), 'edge_att': nrm(ks[2], (E, EDGE_D)), 'W0': nrm(ks[3], (IN_D, HEADS * H_D), 1.0 / np.sqrt(IN_D)), 'We0': nrm(ks[4], (EDGE_D, HEADS * H_D), 1.0 / np.sqrt(EDGE_D)), 'as0': nrm(ks[5], (1, HEADS, H_D), 0.1), 'ad0': nrm(ks[6], (1, HEADS, H_D), 0.1), 'ae0': nrm(ks[7], (1, HEADS, H_D), 0.1), 'b0': jnp.zeros((H_D,), jnp.float32), 'g0': jnp.ones((H_D,), jnp.float32), 'beta0': jnp.zeros((H_D,), jnp.float32), 'W1': nrm(ks[8], (H_D, HEADS * OUT_D), 1.0 / np.sqrt(H_D)), 'We1': nrm(ks[9], (EDGE_D, HEADS * OUT_D), 1.0 / np.sqrt(EDGE_D)), 'as1': nrm(ks[10], (1, HEADS, OUT_D), 0.1), 'ad1': nrm(ks[11], (1, HEADS, OUT_D), 0.1), 'ae1': nrm(ks[12], (1, HEADS, OUT_D), 0.1), 'b1': jnp.zeros((OUT_D,), jnp.float32), 'gf': jnp.ones((OUT_D,), jnp.float32), 'betaf': jnp.zeros((OUT_D,), jnp.float32)}
        return inp
    _L1_gnn_all = _L1_gnn_setup()
    _L1_gnn_in = {k: v for k, v in _L1_gnn_all.items() if k in ('W0', 'We0', 'as0', 'ad0', 'ae0', 'b0', 'g0', 'beta0', 'W1', 'We1', 'as1', 'ad1', 'ae1', 'b1', 'gf', 'betaf')}
    del _L1_gnn_all
    return {'x': x, 'src': src, 'dst': dst, 'edge_attr_16': edge_attr_16, 'L0_gnn_Wf1': _L0_gnn_in['Wf1'], 'L0_gnn_bf1': _L0_gnn_in['bf1'], 'L0_gnn_Ws1': _L0_gnn_in['Ws1'], 'L0_gnn_bs1': _L0_gnn_in['bs1'], 'L0_gnn_Wf2': _L0_gnn_in['Wf2'], 'L0_gnn_bf2': _L0_gnn_in['bf2'], 'L0_gnn_Ws2': _L0_gnn_in['Ws2'], 'L0_gnn_bs2': _L0_gnn_in['bs2'], 'L1_gnn_W0': _L1_gnn_in['W0'], 'L1_gnn_We0': _L1_gnn_in['We0'], 'L1_gnn_as0': _L1_gnn_in['as0'], 'L1_gnn_ad0': _L1_gnn_in['ad0'], 'L1_gnn_ae0': _L1_gnn_in['ae0'], 'L1_gnn_b0': _L1_gnn_in['b0'], 'L1_gnn_g0': _L1_gnn_in['g0'], 'L1_gnn_beta0': _L1_gnn_in['beta0'], 'L1_gnn_W1': _L1_gnn_in['W1'], 'L1_gnn_We1': _L1_gnn_in['We1'], 'L1_gnn_as1': _L1_gnn_in['as1'], 'L1_gnn_ad1': _L1_gnn_in['ad1'], 'L1_gnn_ae1': _L1_gnn_in['ae1'], 'L1_gnn_b1': _L1_gnn_in['b1'], 'L1_gnn_gf': _L1_gnn_in['gf'], 'L1_gnn_betaf': _L1_gnn_in['betaf']}

def reference(x, src, dst, edge_attr_16, L0_gnn_Wf1, L0_gnn_bf1, L0_gnn_Ws1, L0_gnn_bs1, L0_gnn_Wf2, L0_gnn_bf2, L0_gnn_Ws2, L0_gnn_bs2, L1_gnn_W0, L1_gnn_We0, L1_gnn_as0, L1_gnn_ad0, L1_gnn_ae0, L1_gnn_b0, L1_gnn_g0, L1_gnn_beta0, L1_gnn_W1, L1_gnn_We1, L1_gnn_as1, L1_gnn_ad1, L1_gnn_ae1, L1_gnn_b1, L1_gnn_gf, L1_gnn_betaf):
    import jax
    import jax.numpy as jnp

    def _L0_gnn_ref(x, edge_index, Wf1, bf1, Ws1, bs1, Wf2, bf2, Ws2, bs2):
        import jax, jax.numpy as jnp
        import numpy as np
        N = 6250
        E = 100000
        C = 64

        def _linear_params(key, fan_in, fan_out):
            kw, kb = jax.random.split(key)
            s = 1.0 / np.sqrt(fan_in)
            W = jax.random.uniform(kw, (fan_in, fan_out), jnp.float32, -s, s)
            b = jax.random.uniform(kb, (fan_out,), jnp.float32, -s, s)
            return (W, b)

        def _cgconv(x, edge_index, Wf, bf, Ws, bs):
            j, i = (edge_index[0], edge_index[1])
            z = jnp.concatenate([x[i], x[j]], axis=-1)
            m = jax.nn.sigmoid(z @ Wf + bf) * jax.nn.softplus(z @ Ws + bs)
            agg = jax.ops.segment_sum(m, i, num_segments=x.shape[0])
            return x + agg
        h = jax.nn.relu(_cgconv(x, edge_index, Wf1, bf1, Ws1, bs1))
        return jax.nn.relu(_cgconv(h, edge_index, Wf2, bf2, Ws2, bs2))

    def _L1_gnn_ref(x, edge_index, edge_att, W0, We0, as0, ad0, ae0, b0, g0, beta0, W1, We1, as1, ad1, ae1, b1, gf, betaf):
        import jax, jax.numpy as jnp
        import numpy as np
        N = 12500
        E = 200000
        IN_D = 64
        H_D = 64
        OUT_D = 64
        EDGE_D = 16
        HEADS = 1
        NEG_SLOPE = 0.2
        BN_EPS = 1e-05

        def gat_conv(x, src, dst, edge_attr, W, We, att_s, att_d, att_e, bias):
            n = x.shape[0]
            C = W.shape[1] // HEADS
            deg = jax.ops.segment_sum(jnp.ones((src.shape[0],), x.dtype), dst, num_segments=n)
            loop_attr = jax.ops.segment_sum(edge_attr, dst, num_segments=n) / jnp.clip(deg, 1.0)[:, None]
            src2 = jnp.concatenate([src, jnp.arange(n, dtype=src.dtype)])
            dst2 = jnp.concatenate([dst, jnp.arange(n, dtype=dst.dtype)])
            ea2 = jnp.concatenate([edge_attr, loop_attr], axis=0)
            xl = (x @ W).reshape(n, HEADS, C)
            a_src = (xl * att_s).sum(-1)
            a_dst = (xl * att_d).sum(-1)
            el = (ea2 @ We).reshape(-1, HEADS, C)
            a_edge = (el * att_e).sum(-1)
            alpha = a_src[src2] + a_dst[dst2] + a_edge
            alpha = jax.nn.leaky_relu(alpha, NEG_SLOPE)
            amax = jax.ops.segment_max(alpha, dst2, num_segments=n)
            ex = jnp.exp(alpha - amax[dst2])
            den = jax.ops.segment_sum(ex, dst2, num_segments=n)
            p = ex / den[dst2]
            out = jax.ops.segment_sum(xl[src2] * p[..., None], dst2, num_segments=n)
            return out.mean(axis=1) + bias

        def batch_norm(h, gamma, beta):
            m = h.mean(axis=0)
            v = h.var(axis=0)
            return gamma * (h - m) * jax.lax.rsqrt(v + BN_EPS) + beta
        src, dst = (edge_index[0], edge_index[1])
        h = gat_conv(x, src, dst, edge_att, W0, We0, as0, ad0, ae0, b0)
        h = batch_norm(h, g0, beta0)
        h = jax.nn.relu(h)
        h = gat_conv(h, src, dst, edge_att, W1, We1, as1, ad1, ae1, b1)
        h = batch_norm(h, gf, betaf)
        return h
    edge_index = jnp.stack([src, dst])
    x = _layernorm(x + _L0_gnn_ref(x, edge_index, L0_gnn_Wf1, L0_gnn_bf1, L0_gnn_Ws1, L0_gnn_bs1, L0_gnn_Wf2, L0_gnn_bf2, L0_gnn_Ws2, L0_gnn_bs2), axis=-1)
    x = _layernorm(x + _L1_gnn_ref(x, edge_index, edge_attr_16, L1_gnn_W0, L1_gnn_We0, L1_gnn_as0, L1_gnn_ad0, L1_gnn_ae0, L1_gnn_b0, L1_gnn_g0, L1_gnn_beta0, L1_gnn_W1, L1_gnn_We1, L1_gnn_as1, L1_gnn_ad1, L1_gnn_ae1, L1_gnn_b1, L1_gnn_gf, L1_gnn_betaf), axis=-1)
    return x

_drawn_inputs = setup_inputs


def setup_inputs(seed=0):
    import zlib

    import numpy as np

    out = dict(_drawn_inputs(seed))
    spreads = {'L1_gnn_b0': (0.0, 0.8),
     'L1_gnn_g0': (1.0, 0.2),
     'L1_gnn_beta0': (0.0, 0.1),
     'L1_gnn_b1': (0.0, 0.8),
     'L1_gnn_gf': (1.0, 0.2),
     'L1_gnn_betaf': (0.0, 0.1)}
    factors = {'L0_gnn_bf2': 3.164}
    for name, (base, spread) in spreads.items():
        noise = np.random.default_rng([zlib.crc32(name.encode()), seed]).standard_normal(out[name].shape)
        drawn = base * np.exp(spread * noise) if base else spread * noise
        out[name] = jnp.asarray(drawn.astype(out[name].dtype))
    for name, factor in factors.items():
        out[name] = (out[name] * factor).astype(out[name].dtype)
    return out
```

```python
from contextlib import ExitStack

import concourse.bass as bass
from concourse import mybir
from concourse.alu_op_type import AluOpType as ALU

F32 = mybir.dt.float32
BF16 = mybir.dt.bfloat16
I32 = mybir.dt.int32
ACT = mybir.ActivationFunctionType
AX = mybir.AxisListType
ds = bass.ds

P = 128
N = 12500
E = 200000
C = 64
D = 16
NB = -(-N // P)
LAST = N - (NB - 1) * P
TILES = -(-E // P)
FULL = E // P
NBATCH = -(-(TILES + NB - 1) // P)
STEPS = NBATCH * P
GROUP = 4
UNROLL = 4
ITER = GROUP * UNROLL
GROUPS = STEPS // GROUP
BGROUPS = P // GROUP
CH = NBATCH
PAD = 32768.0
BIG_NEG = -1.0e30
AW = C + 3
TW = C + 1
HALF = P // 2
RING = UNROLL * GROUP * 2 * C
BIG = NB * 2 * C + RING
PREV, KEY, NEXT, SRC, AE = 0, 1, 1 + P, 2 + P, 2 + 2 * P
RW = AE + 2 * P
SLOPE = 0.2
EPS = 1e-5


def wait(eng, sem, value):
    if isinstance(value, int) and value <= 0:
        return
    eng.wait_ge(sem, value)


def flat(ap):
    return ap.rearrange("p o c -> p (o c)")


class Core:

    def __init__(self, nc, ctx):
        self.nc, self.ctx = nc, ctx
        self.old, self.cur = None, (ExitStack(), [])
        self.setup_rows = [ctx.enter_context(nc.semaphore(f"setup_rows{i}")) for i in range(2)]
        self.rows = [ctx.enter_context(nc.semaphore(f"rows{i}")) for i in range(4)]
        self.row_base = [0] * 4

        def sb(name, shape, dt=F32):
            return ctx.enter_context(nc.sbuf_tensor(name, shape, dt))

        self.sb = sb
        self.big = sb("big", [P, BIG + NB * C])
        self.node_a = self.big[:, BIG:BIG + NB * C].rearrange("p (b c) -> p b c", c=C)
        self.wide = sb("wide", [P, NB * C + NB * AW])
        self.node_b = self.wide[:, 0:NB * C].rearrange("p (b c) -> p b c", c=C)
        self.acc = self.wide[:, NB * C:NB * (C + AW)].rearrange("p (b c) -> p b c", c=AW)
        self.src_idx = sb("src_idx", [P, STEPS + HALF], I32)
        self.dst_rel = sb("dst_rel", [P, STEPS])
        self.ae = sb("ae", [P, STEPS, 2])
        self.keys = sb("keys", [P, NBATCH * (P + 2)])
        self.block_row = sb("block_row", [1, STEPS], I32)
        self.idx_stage = sb("idx_stage", [P, P], I32)
        self.onehot = sb("onehot", [P, UNROLL, GROUP, P])
        self.onehot_t = sb("onehot_t", [P, 2, GROUP, P])
        self.msg = sb("msg", [P, UNROLL, GROUP, AW])
        self.work = sb("work", [P, 18 * P + 16])
        self.ident = sb("ident", [P, P])
        self.iota = sb("iota", [P, P])
        self.iota_col = sb("iota_col", [P, 1])
        self.ones_row = sb("ones_row", [1, P])
        self.ones_sq = sb("ones_sq", [P, P])
        self.row_mask = sb("row_mask", [P, 1])
        self.loop_sum = sb("loop_sum", [P, NB, 3])
        self.small = sb("small", [P, NB * 6])
        self.spread = self.small[:, 0:2 * NB].rearrange("p (b j) -> p b j", j=2)
        self.node_col = self.small[:, 2 * NB:6 * NB].rearrange("p (j b) -> p j b", b=NB)
        self.wc = self.small[0:C + 1, 0:8 * C].rearrange("p (l c) -> p l c", l=2)
        self.xt = sb("xt", [C + 1, 2, P])
        self.gw = sb("gw", [C, 2, C + 2])
        self.gvec = sb("gvec", [P, 6, C])
        self.psum = [ctx.enter_context(nc.psum_tensor(f"bank{i}", [P, 512], F32)) for i in range(8)]
        self.edge_rows = nc.dram_tensor("edge_rows", (NBATCH * P, RW), F32, kind="Internal").ap()
        self.q_table = nc.dram_tensor("q_table", (NB * P, 2 * C), F32, kind="Internal").ap()
        self.xl_table = nc.dram_tensor("xl_table", (NB * P, TW), F32, kind="Internal").ap()
        self.x1_dram = nc.dram_tensor("x1_dram", (NB * P, C), F32, kind="Internal").ap()

    def next_stage(self):
        if self.old is not None:
            self.old[0].close()
        self.old, self.cur = self.cur, (ExitStack(), [])

    def sem(self, name):
        handle = self.cur[0].enter_context(self.nc.semaphore(name))
        self.cur[1].append(handle)
        return handle

    def clear_old(self, sp):
        for handle in self.old[1]:
            sp.sem_clear(handle)

    def close(self):
        self.old[0].close()
        self.cur[0].close()


class Chain:

    def __init__(self, eng, sem, base=0):
        self.eng, self.sem, self.base, self.n = eng, sem, base, 0

    def __call__(self, ins):
        self.n += 1
        ins.then_inc(self.sem, 1)
        self.eng.wait_ge(self.sem, self.base + self.n)


def load_nodes(eng, dst, x, sem):
    full = (NB - 1) * P
    eng.dma_start(dst[:, 0:NB - 1, :], x[0:full, :].rearrange("(b p) c -> p b c", p=P)).then_inc(sem, 16)
    eng.dma_start(dst[0:LAST, NB - 1, :], x[full:N, :]).then_inc(sem, 16)


def setup(k, a):
    nc = k.nc
    k.next_stage()
    s_const, s_pad, s_int = k.sem("set_const"), k.sem("set_pad"), k.sem("set_int")
    s_w, s_x, s_ea = k.sem("set_weights"), k.sem("set_x"), [k.sem("set_ea0"), k.sem("set_ea1")]
    s_rows, s_thr, s_cmp, s_cnt = k.sem("set_rows"), k.sem("set_thr"), k.sem("set_cmp"), k.sem("set_cnt")
    s_trow, s_tcol, s_tidx = k.sem("set_trow"), k.sem("set_tcol"), k.sem("set_tidx")
    s_prod, s_red, s_store = k.sem("set_prod"), k.sem("set_red"), k.sem("set_store")
    s_g, s_rel, s_tr, s_out = k.setup_rows, k.sem("set_rel"), k.sem("set_tr"), k.sem("set_out")
    s_wt, s_wtc, s_wv, s_wvc = k.sem("set_wt"), k.sem("set_wtc"), k.sem("set_wv"), k.sem("set_wvc")
    s_ch = k.sem("set_chain")

    rows = k.big[:, 0:CH * RW].rearrange("p (c w) -> p c w", w=RW)
    at = CH * RW
    dint = k.big[:, at:at + CH * P].bitcast(I32).rearrange("p (c e) -> p c e", e=P)
    at += CH * P
    sint = k.big[:, at:at + CH * P].bitcast(I32).rearrange("p (c e) -> p c e", e=P)
    at += CH * P
    ea = [k.big[:, at + i * P * D:at + (i + 1) * P * D].rearrange("p (e d) -> p e d", d=D) for i in range(2)]
    prod = k.wide[:, 8000:8000 + P * D].rearrange("p (e d) -> p e d", d=D)
    neigh = k.work[:, 0:2 * CH].bitcast(I32).rearrange("p (c w) -> p c w", w=2)
    blk = k.work[:, 32:32 + CH].bitcast(I32)
    thr = k.work[:, 48:48 + CH]
    tile1 = k.work[:, 64:64 + CH]
    step_col = k.work[:, 80:80 + CH]
    tcol = k.work[:, 96:96 + CH]
    tidx = k.work[:, 112:112 + CH].bitcast(I32)
    off = k.work[:, 128:128 + CH]
    ones_bf = k.work[:, 144:145].bitcast(BF16)[:, 0:1]
    vb = k.work[:, 160:160 + 2 * D].rearrange("p (l d) -> p l d", d=D)
    wet = k.work[0:C, 192:192 + 2 * D].rearrange("p (l d) -> p l d", d=D)
    att = k.work[0:C, 224:230]
    aeb = k.work[0:C, 256:512].rearrange("p (l e) -> p l e", e=P)
    wt = k.work[0:C, 512:512 + 2 * C].rearrange("p (l c) -> p l c", c=C)
    we = k.work[0:D, 640:640 + 2 * C].rearrange("p (l c) -> p l c", c=C)
    t_row = k.wide[0:1, 0:STEPS]
    b_row = k.wide[0:1, STEPS:2 * STEPS]
    iota_s = k.wide[:, 2 * STEPS:3 * STEPS]
    cmp = [k.wide[:, 3 * STEPS + i * STEPS // 2:3 * STEPS + (i + 1) * STEPS // 2].bitcast(BF16) for i in range(2)]
    at = 4 * STEPS
    gath = [k.wide[:, at + i * RW:at + (i + 1) * RW] for i in range(2)]
    at += 2 * RW
    rel = [k.wide[:, at + i * P:at + (i + 1) * P] for i in range(2)]
    part = FULL - (CH - 1) * P
    tail = E - FULL * P
    NCONST, NRED = 12, 2

    with nc.Block() as block:
        @block.gpsimd
        def _(pool):
            nc.gpsimd.memset(rows[:, CH - 1, :], 0.0).then_inc(s_pad, 1)
            nc.gpsimd.memset(dint[:, CH - 1, :], int(PAD)).then_inc(s_pad, 1)
            nc.gpsimd.memset(sint[:, CH - 1, :], 0).then_inc(s_pad, 1)
            nc.gpsimd.memset(k.src_idx[:, STEPS:STEPS + HALF], 0)
            nc.gpsimd.memset(neigh, -1).then_inc(s_pad, 1)
            nc.gpsimd.memset(k.node_a[:, NB - 1, :], 0.0).then_inc(s_pad, 1)
            nc.gpsimd.iota(tile1, pattern=[[P, CH]], base=1, channel_multiplier=1, allow_small_or_imprecise_dtypes=True).then_inc(s_const, 1)
            nc.gpsimd.iota(iota_s, pattern=[[1, STEPS]], base=0, channel_multiplier=0, allow_small_or_imprecise_dtypes=True).then_inc(s_const, 1)
            nc.gpsimd.memset(ones_bf, 1.0).then_inc(s_const, 1)
            nc.gpsimd.memset(k.ident[:, :], 0.0).then_inc(s_const, 1)
            nc.gpsimd.memset(k.row_mask[:, :], 1.0).then_inc(s_const, 1)
            nc.gpsimd.iota(k.iota[:, :], pattern=[[1, P]], base=0, channel_multiplier=0, allow_small_or_imprecise_dtypes=True).then_inc(s_const, 1)
            nc.gpsimd.iota(k.iota_col[:, :], pattern=[[0, 1]], base=0, channel_multiplier=1, allow_small_or_imprecise_dtypes=True).then_inc(s_const, 1)
            nc.gpsimd.iota(step_col, pattern=[[P, CH]], base=0, channel_multiplier=1, allow_small_or_imprecise_dtypes=True).then_inc(s_const, 1)
            nc.gpsimd.memset(k.ones_row[:, :], 1.0).then_inc(s_const, 1)
            nc.gpsimd.memset(k.ones_sq[:, :], 1.0).then_inc(s_const, 1)
            pool.wait_ge(s_const, 10)
            nc.gpsimd.affine_select(out=k.ident[:, :], in_=k.ident[:, :], compare_op=ALU.not_equal, fill=1.0,
                                    base=0, pattern=[[-1, P]], channel_multiplier=1).then_inc(s_const, 1)
            nc.gpsimd.affine_select(out=k.row_mask[:, :], in_=k.row_mask[:, :], compare_op=ALU.is_ge, fill=0.0,
                                    base=LAST - 1, pattern=[[0, 1]], channel_multiplier=-1).then_inc(s_const, 1)
            pool.wait_ge(s_store, 16)
            pool.wait_ge(s_tidx, 1)
            for b in range(NBATCH):
                if b >= 2:
                    pool.wait_ge(s_rel, 2 * (b - 1))
                    pool.wait_ge(s_tr, b - 1)
                pool.indirect_dma_start(out=gath[b % 2], out_offset=None, in_=k.edge_rows,
                                        in_offset=bass.IndirectOffsetOnAxis(ap=tidx[:, b:b + 1], axis=0)).then_inc(s_g[b % 2], 16)

        @block.sync
        def _(sp):
            k.clear_old(sp)
            with nc.allow_non_contiguous_dma(reason="one neighbouring key per tile"):
                sp.wait_ge(s_pad, 7)
                head = (CH - 1) * P
                for src, dst in ((a["dst"], dint), (a["src"], sint)):
                    sp.dma_start(dst[:, 0:CH - 1, :], src[0:head * P].rearrange("(c p e) -> p c e", p=P, e=P)).then_inc(s_int, 16)
                    sp.dma_start(dst[0:part, CH - 1, :], src[head * P:FULL * P].rearrange("(p e) -> p e", e=P)).then_inc(s_int, 16)
                    sp.dma_start(dst[part:part + 1, CH - 1, 0:tail], src[FULL * P:E].rearrange("(p e) -> p e", p=1)).then_inc(s_int, 16)
                by_tile = a["dst"][0:FULL * P].rearrange("(t e) -> t e", e=P)
                for c in range(CH):
                    lo = 1 if c == 0 else 0
                    hi = P if c < CH - 1 else part + 1
                    sp.dma_start(neigh[lo:hi, c, 0:1], by_tile[c * P + lo - 1:c * P + hi - 1, P - 1:P]).then_inc(s_int, 16)
                    hi = P if c < CH - 1 else part - 1
                    sp.dma_start(neigh[0:hi, c, 1:2], by_tile[c * P + 1:c * P + 1 + hi, 0:1]).then_inc(s_int, 16)
                sp.dma_start(neigh[part - 1:part, CH - 1, 1:2], a["dst"][FULL * P:FULL * P + 1].rearrange("(p e) -> p e", p=1)).then_inc(s_int, 16)
            load_nodes(sp, k.node_a, a["x"], s_x)
            sp.wait_ge(s_rows, 1)
            sp.wait_ge(s_red, NRED * CH + 1)
            sp.dma_start(k.edge_rows.rearrange("(c p) w -> p c w", p=P), rows).then_inc(s_store, 16)
            sp.wait_ge(s_store, 16)
            sp.wait_ge(s_x, 32)

        @block.scalar
        def _(act):
            n = 0
            def w(out, in_):
                act.dma_start(out, in_).then_inc(s_w, 16)
            act.wait_ge(s_pad, 7)
            for l, we_n in enumerate(("L1_gnn_We0", "L1_gnn_We1")):
                w(we[:, l, :], a[we_n])
                w(k.gw[:, l, 0:C], a[f"L1_gnn_W{l}"])
                for j, v in enumerate(("as", "ad", "ae")):
                    w(att[:, 3 * l + j:3 * l + j + 1], a[f"L1_gnn_{v}{l}"].rearrange("a h c -> c (a h)"))
            for l in range(2):
                for h, m in enumerate("fs"):
                    big = a[f"L0_gnn_W{m}{l + 1}"]
                    w(k.wc[0:C, l, h * C:(h + 1) * C], big[0:C, :])
                    w(k.wc[0:C, l, (2 + h) * C:(3 + h) * C], big[C:2 * C, :])
                    w(k.wc[C:C + 1, l, h * C:(h + 1) * C], a[f"L0_gnn_b{m}{l + 1}"].rearrange("(p c) -> p c", p=1))
            for j, v in enumerate(("b0", "g0", "beta0", "b1", "gf", "betaf")):
                act.dma_start(k.gvec[:, j, :], a["L1_gnn_" + v].rearrange("(p c) -> p c", p=1).broadcast_to([P, C])).then_inc(s_w, 16)
            for c in range(CH):
                if c >= 2:
                    act.wait_ge(s_red, NRED * (c - 1))
                t0 = c * P
                if c < CH - 1:
                    act.dma_start(ea[c % 2], a["edge_attr_16"][t0 * P:(t0 + P) * P, :].rearrange("(p e) d -> p e d", e=P)).then_inc(s_ea[c % 2], 16)
                else:
                    act.wait_ge(s_red, NRED * c + 1)
                    act.dma_start(ea[c % 2][0:part], a["edge_attr_16"][t0 * P:FULL * P, :].rearrange("(p e) d -> p e d", e=P)).then_inc(s_ea[c % 2], 16)
                    act.dma_start(ea[c % 2][part:part + 1, 0:tail, :], a["edge_attr_16"][FULL * P:E, :].rearrange("(p e) d -> p e d", p=1)).then_inc(s_ea[c % 2], 16)
            act.wait_ge(s_w, 16 * (10 + 12 + 6))
            for b in range(NBATCH):
                act.wait_ge(s_tr, b + 1)
                bank = k.psum[b % 2]
                nc.scalar.activation(k.dst_rel[:, b * P:(b + 1) * P], bank[:, 0:P], ACT.Copy).then_inc(s_out, 1)
                for l in range(2):
                    nc.scalar.activation(k.ae[:, b * P:(b + 1) * P, l], bank[:, (2 + l) * P:(3 + l) * P], ACT.Copy).then_inc(s_out, 1)

        @block.vector
        def _(v):
            link = Chain(v, s_ch)
            nc.vector.memset(k.wc[C:C + 1, :, :], 0.0).then_inc(s_pad, 1)
            nc.vector.memset(k.xt[C:C + 1, :, :], 1.0).then_inc(s_pad, 1)
            v.wait_ge(s_const, NCONST)
            v.wait_ge(s_w, 16 * (10 + 12 + 6))
            for l in range(2):
                link(nc.vector.tensor_copy(aeb[:, l, :], att[:, 3 * l + 2:3 * l + 3].broadcast_to([C, P])))
            v.wait_ge(s_wt, 1)
            nc.vector.tensor_copy(wet.rearrange("p l d -> p (l d)"), k.psum[7][0:C, 0:2 * D]).then_inc(s_wtc, 1)
            nc.vector.tensor_copy(wt.rearrange("p l c -> p (l c)"), k.psum[7][0:C, P:P + 2 * C]).then_inc(s_wtc, 1)
            v.wait_ge(s_wv, 1)
            link(nc.vector.tensor_copy(vb.rearrange("p l d -> p (l d)"), k.psum[6][:, 0:2 * D]))
            for l in range(2):
                link(nc.vector.tensor_copy(k.gw[:, l, C:C + 2], k.psum[6][0:C, P + 2 * l:P + 2 * l + 2]))
            v.wait_ge(s_int, 16 * (6 + 2 * CH + 1))
            link(nc.vector.tensor_scalar(blk, dint[:, :, P - 1], 7, None, ALU.arith_shift_right))
            link(nc.vector.tensor_copy(thr, blk))
            nc.vector.tensor_tensor(thr, thr, tile1, ALU.add).then_inc(s_thr, 1)
            v.wait_ge(s_thr, 1)
            for c in range(CH):
                if c >= 2:
                    v.wait_ge(s_cnt, c - 1)
                nc.vector.tensor_scalar(cmp[c % 2], iota_s, thr[:, c:c + 1], None, ALU.is_ge).then_inc(s_cmp, 1)
            nc.vector.tensor_copy(rows[:, :, KEY:KEY + P], dint)
            nc.vector.tensor_copy(rows[:, :, SRC:SRC + P], sint)
            nc.vector.tensor_copy(rows[:, :, PREV:PREV + 1], neigh[:, :, 0:1])
            nc.vector.tensor_copy(rows[:, :, NEXT:NEXT + 1], neigh[:, :, 1:2]).then_inc(s_rows, 1)
            v.wait_ge(s_cnt, CH)
            for j in range(4):
                link(nc.vector.tensor_copy(t_row[:, j * STEPS // 4:(j + 1) * STEPS // 4], k.psum[2 + j][0:1, 0:STEPS // 4]))
            nc.vector.tensor_tensor(b_row, iota_s[0:1, :], t_row, ALU.subtract).then_inc(s_trow, 1)
            v.wait_ge(s_trow, 1)
            link(nc.vector.tensor_scalar(k.block_row[:, :], b_row, float(NB - 1), None, ALU.min))
            v.wait_ge(s_tcol, 1)
            link(nc.vector.tensor_copy(tcol, k.psum[6][:, 256:256 + CH]))
            nc.vector.tensor_copy(tidx, tcol).then_inc(s_tidx, 1)
            link(nc.vector.tensor_tensor(off, step_col, tcol, ALU.subtract))
            link(nc.vector.tensor_scalar(off, off, float(P), None, ALU.mult))
            for c in range(CH):
                if c == CH - 1:
                    v.wait_ge(s_red, NRED * c)
                    nc.vector.memset(ea[c % 2], 0.0).then_inc(s_red, 1)
                    v.wait_ge(s_ea[c % 2], 16 * (c // 2) + 32)
                else:
                    v.wait_ge(s_ea[c % 2], 16 * (c // 2 + 1))
                for l in range(2):
                    done = 2 * c + l
                    wait(v, s_red, done + (c == CH - 1))
                    nc.vector.tensor_tensor(prod, ea[c % 2], vb[:, l, :].unsqueeze(1).broadcast_to([P, P, D]), ALU.mult).then_inc(s_prod, 1)
                    v.wait_ge(s_prod, done + 1)
                    nc.vector.tensor_reduce(rows[:, c, AE + l * P:AE + (l + 1) * P], prod, AX.X, ALU.add).then_inc(s_red, 1)
            for b in range(NBATCH):
                v.wait_ge(s_g[b % 2], 16 * (b // 2 + 1))
                nc.vector.tensor_copy(k.keys[:, b * (P + 2):(b + 1) * (P + 2)], gath[b % 2][:, 0:P + 2]).then_inc(s_rel, 1)
                wait(v, s_tr, b - 1)
                nc.vector.tensor_scalar(rel[b % 2], gath[b % 2][:, KEY:KEY + P], off[:, b:b + 1], None, ALU.subtract).then_inc(s_rel, 1)
                v.wait_ge(s_tr, b + 1)
                v.wait_ge(s_out, 4 * b + 3)
                nc.vector.tensor_copy(k.src_idx[:, b * P:(b + 1) * P], k.psum[b % 2][:, P:2 * P]).then_inc(s_out, 1)

        @block.tensor
        def _(pe):
            pe.wait_ge(s_const, NCONST)
            pe.wait_ge(s_w, 16 * (10 + 12 + 6))
            for l in range(2):
                nc.tensor.transpose(k.psum[7][0:C, l * D:(l + 1) * D], we[:, l, :], k.ident[0:D, 0:D])
            for l in range(2):
                last = nc.tensor.transpose(k.psum[7][0:C, P + l * C:P + (l + 1) * C], k.gw[:, l, 0:C], k.ident[0:C, 0:C])
            last.then_inc(s_wt, 1)
            pe.wait_ge(s_wtc, 2)
            pe.wait_ge(s_ch, 2)
            for l in range(2):
                nc.tensor.matmul(k.psum[6][:, l * D:(l + 1) * D], aeb[:, l, :], wet[:, l, :], start=True, stop=True)
            for l in range(2):
                last = nc.tensor.matmul(k.psum[6][0:C, P + 2 * l:P + 2 * l + 2], wt[:, l, :], att[:, 3 * l:3 * l + 2], start=True, stop=True)
            last.then_inc(s_wv, 1)
            for c in range(CH):
                pe.wait_ge(s_cmp, c + 1)
                for j in range(4):
                    w = STEPS // 4
                    last = nc.tensor.matmul(k.psum[2 + j][0:1, 0:w], ones_bf, cmp[c % 2][:, j * w:(j + 1) * w], start=c == 0, stop=c == CH - 1)
                last.then_inc(s_cnt, 1)
            pe.wait_ge(s_trow, 1)
            pe.wait_ge(s_ch, 5)
            for b in range(NBATCH):
                last = nc.tensor.transpose(k.psum[6][:, 256 + b:257 + b], t_row[:, b * P:(b + 1) * P], k.ident[0:1, 0:1])
            last.then_inc(s_tcol, 1)
            for b in range(NBATCH):
                pe.wait_ge(s_g[b % 2], 16 * (b // 2 + 1))
                pe.wait_ge(s_rel, 2 * b + 2)
                wait(pe, s_out, 4 * (b - 1))
                g = gath[b % 2]
                for j, m in enumerate((rel[b % 2], g[:, SRC:SRC + P], g[:, AE:AE + P], g[:, AE + P:AE + 2 * P])):
                    last = nc.tensor.transpose(k.psum[b % 2][:, j * P:(j + 1) * P], m, k.ident[:, :])
                last.then_inc(s_tr, 1)


def cg_tables(k, layer):
    nc = k.nc
    k.next_stage()
    n = f"cgt{layer}_"
    s_z, s_h, s_t, s_tc, s_m, s_p, s_q, s_st = (k.sem(n + x) for x in ("zero", "h", "t", "tc", "m", "p", "q", "store"))
    p_tab = k.big[:, 0:NB * 2 * C]
    q_stage = k.wide[:, 0:NB * 2 * C]
    q_rows = k.q_table.rearrange("(b p) c -> p b c", p=P)

    h_stage = k.work[:, 0:2 * P].rearrange("p (j c) -> p j c", c=P)

    with nc.Block() as block:
        @block.gpsimd
        def _(pool):
            def body(b, j):
                wait(pool, s_t, b - 1)
                nc.gpsimd.tensor_copy(h_stage[:, j, 0:C], flat(k.node_a[:, ds(b, 1), :])).then_inc(s_h, 1)
            nc.gpsimd.memset(k.work[:, 0:2 * P], 0.0).then_inc(s_z, 1)
            pool.wait_ge(s_z, 1)
            body(0, 0)
            body(1, 1)
            with pool.Fori(1, NB // 2) as i:
                body(i * 2, 0)
                body(i * 2 + 1, 1)

        @block.tensor
        def _(pe):
            def body(b, j):
                pe.wait_ge(s_h, b + 1)
                wait(pe, s_tc, b - 1)
                nc.tensor.transpose(k.psum[j][:, 0:P], h_stage[:, j, :], k.ident[:, :]).then_inc(s_t, 1)
                pe.wait_ge(s_tc, b + 1)
                wait(pe, s_p, b - 1)
                wait(pe, s_q, b - 1)
                nc.tensor.matmul(k.psum[2 + j][:, 0:4 * C], k.xt[:, j, :], k.wc[:, layer, :], start=True, stop=True).then_inc(s_m, 1)
            body(0, 0)
            body(1, 1)
            with pe.Fori(1, NB // 2) as i:
                body(i * 2, 0)
                body(i * 2 + 1, 1)

        @block.scalar
        def _(act):
            def body(b, j):
                act.wait_ge(s_t, b + 1)
                wait(act, s_m, b - 1)
                nc.scalar.activation(k.xt[0:C, j, :], k.psum[j][0:C, 0:P], ACT.Copy).then_inc(s_tc, 1)
                act.wait_ge(s_m, b + 1)
                nc.scalar.activation(p_tab[:, ds(b * 2 * C, 2 * C)], k.psum[2 + j][:, 0:2 * C], ACT.Copy).then_inc(s_p, 1)
            body(0, 0)
            body(1, 1)
            with act.Fori(1, NB // 2) as i:
                body(i * 2, 0)
                body(i * 2 + 1, 1)

        @block.vector
        def _(v):
            def body(b, j):
                v.wait_ge(s_p, b + 1)
                nc.vector.tensor_copy(q_stage[:, ds(b * 2 * C, 2 * C)], k.psum[2 + j][:, 2 * C:4 * C]).then_inc(s_q, 1)
            with v.Fori(0, NB // 2) as i:
                body(i * 2, 0)
                body(i * 2 + 1, 1)

        @block.sync
        def _(sp):
            k.clear_old(sp)
            with sp.Fori(0, NB // 14) as i:
                sp.wait_ge(s_q, i * 14 + 14)
                sp.dma_start(q_rows[:, ds(i * 14, 14), :],
                             q_stage[:, ds(i * 14 * 2 * C, 14 * 2 * C)].rearrange("p (b c) -> p b c", c=2 * C)).then_inc(s_st, 16)
            sp.wait_ge(s_st, 16 * (NB // 14))


def build_onehot(k, nc, buf, s):
    return nc.vector.tensor_tensor(k.onehot[:, buf, :, :], k.iota[:, :].unsqueeze(1).broadcast_to([P, GROUP, P]),
                                   k.dst_rel[:, ds(s, GROUP)].unsqueeze(2).broadcast_to([P, GROUP, P]), ALU.is_equal)


def load_blocks(k, eng, s):
    return [eng.value_load(k.block_row[0:1, ds(s + i, 1)], min_val=0, max_val=NB - 1) for i in range(GROUP)]


def cg_edges(k, layer):
    nc = k.nc
    k.next_stage()
    n = f"cge{layer}_"
    (s_zero, s_S, s_T, s_Tc, s_X, s_pre, s_ln, s_soft, s_sig, s_msg, s_agg, s_acc, s_idx, s_abs) = (
        k.sem(n + x) for x in ("zero", "onehot", "trans", "trans_sb", "spread", "pre", "ln", "soft", "sig", "msg", "agg", "acc", "idx", "abs"))
    s_row, row_base = k.rows, list(k.row_base)
    k.row_base = [r + GROUPS // UNROLL * GROUP * 16 for r in row_base]
    s_turn = k.sem(n + "turn")
    p_tab = k.big[:, 0:NB * 2 * C]
    ring = k.big[:, NB * 2 * C:NB * 2 * C + UNROLL * GROUP * 2 * C].rearrange("p (u i c) -> p u i c", u=UNROLL, c=2 * C)
    pre = k.work[:, 0:8 * P].rearrange("p (u i c) -> p u i c", u=2, c=2 * C)
    soft = k.work[:, 8 * P:16 * P].rearrange("p (u i c) -> p u i c", u=2, c=2 * C)
    width = AW if layer == 0 else C
    ITERS = GROUPS // UNROLL

    with nc.Block() as block:
        @block.sync
        def _(sp):
            k.clear_old(sp)

        @block.gpsimd
        def _(pool):
            def batch(b):
                for s in range(P):
                    u = s // GROUP % UNROLL
                    if s % GROUP == 0:
                        wait(pool, s_pre, b * BGROUPS + s // GROUP - UNROLL + 1)
                        pool.sem_inc(s_turn, 1)
                    if s % HALF == HALF // 2:
                        start = b * P + (HALF if s < HALF else P)
                        other = (HALF if s < HALF else 0)
                        nc.gpsimd.tensor_copy(k.idx_stage[:, other:other + HALF], k.src_idx[:, ds(start, HALF)]).then_inc(s_idx, 1)
                    if s % HALF == 0:
                        pool.wait_ge(s_idx, b * 2 + s // HALF + 1)
                        pool.sem_inc(s_turn, 1)
                    pool.indirect_dma_start(out=ring[:, u, s % GROUP, :], out_offset=None, in_=k.q_table,
                                            in_offset=bass.IndirectOffsetOnAxis(ap=k.idx_stage[:, s:s + 1], axis=0)).then_inc(s_row[u], 16)
            nc.gpsimd.tensor_copy(k.idx_stage[:, 0:HALF], k.src_idx[:, 0:HALF]).then_inc(s_idx, 1)
            batch(0)
            with pool.Fori(1, NBATCH) as b:
                batch(b)

        @block.vector
        def _(v):
            nc.vector.memset(k.acc, 0.0).then_inc(s_zero, 1)
            if layer == 0:
                nc.vector.memset(k.msg[:, :, :, C + 2:C + 3], 1.0).then_inc(s_zero, 1)

            def onehot(it, u):
                wait(v, s_agg, it * UNROLL + u - 3)
                build_onehot(k, nc, u, it * ITER + u * GROUP).then_inc(s_S, 1)

            def form(it, u):
                g = it * UNROLL + u
                v.wait_ge(s_X, g + 1)
                v.wait_ge(s_row[u], it * (16 * GROUP) + (16 * GROUP + row_base[u]))
                wait(v, s_soft, 2 * g - 2)
                nc.vector.tensor_tensor(pre[:, u % 2], k.psum[2 + u % 2][:, :].rearrange("p (i c) -> p i c", c=2 * C),
                                        ring[:, u], ALU.add).then_inc(s_pre, 1)

            def softs(it, u):
                g = it * UNROLL + u
                v.wait_ge(s_ln, g + 1)
                f, h = slice(0, C), slice(C, 2 * C)
                nc.vector.scalar_tensor_tensor(soft[:, u % 2, :, f], pre[:, u % 2, :, f], 0.0, soft[:, u % 2, :, f], ALU.min, ALU.subtract).then_inc(s_soft, 1)
                nc.vector.scalar_tensor_tensor(soft[:, u % 2, :, h], pre[:, u % 2, :, h], 0.0, soft[:, u % 2, :, h], ALU.max, ALU.add).then_inc(s_soft, 1)

            def message(it, u):
                g = it * UNROLL + u
                v.wait_ge(s_sig, g + 1)
                v.wait_ge(s_soft, 2 * g + 2)
                wait(v, s_agg, g - 3)
                nc.vector.tensor_tensor(k.msg[:, u, :, 0:C], soft[:, u % 2, :, 0:C], soft[:, u % 2, :, C:2 * C], ALU.mult).then_inc(s_msg, 1)

            def accumulate(it, u):
                g = it * UNROLL + u
                blocks = load_blocks(k, v, it * ITER + u * GROUP)
                v.wait_ge(s_agg, g + 1)
                for i in range(GROUP):
                    wait(v, s_acc, g * GROUP + i)
                    to = flat(k.acc[:, ds(blocks[i], 1), 0:width])
                    nc.vector.tensor_tensor(to, to, k.psum[4 + u % 2][:, i * P:i * P + width], ALU.add).then_inc(s_acc, 1)

            def iteration(it):
                for u in range(UNROLL + 3):
                    if u < UNROLL:
                        onehot(it, u)
                    if 0 <= u - 1 < UNROLL:
                        form(it, u - 1)
                    if 0 <= u - 2 < UNROLL:
                        softs(it, u - 2)
                        message(it, u - 2)
                    if 0 <= u - 3 < UNROLL:
                        accumulate(it, u - 3)
            v.wait_ge(s_zero, 1 + (layer == 0))
            iteration(0)
            with v.Fori(1, ITERS) as it:
                iteration(it)

        @block.scalar
        def _(act):
            act.preload_act_table_set("natural_log_exp_and_others")

            def copy_t(it, u):
                g = it * UNROLL + u
                act.wait_ge(s_T, g + 1)
                wait(act, s_X, g - 1)
                nc.scalar.activation(k.onehot_t[:, u % 2, :, :], k.psum[u % 2][:, :].rearrange("p (i c) -> p i c", c=P), ACT.Copy).then_inc(s_Tc, 1)

            def logs(it, u):
                g = it * UNROLL + u
                act.wait_ge(s_pre, g + 1)
                wait(act, s_msg, g - 1)
                nc.scalar.activation(soft[:, u % 2], pre[:, u % 2], ACT.Abs).then_inc(s_abs, 1)
                if layer == 0:
                    wait(act, s_agg, g - 3)
                    nc.scalar.activation(k.msg[:, u, :, C:C + 2], k.ae[:, ds(it * ITER + u * GROUP, GROUP), :], ACT.Copy)
                act.wait_ge(s_abs, 2 * g + 1)
                nc.scalar.activation(soft[:, u % 2], soft[:, u % 2], ACT.Exp, scale=-1.0).then_inc(s_abs, 1)
                act.wait_ge(s_abs, 2 * g + 2)
                nc.scalar.activation(soft[:, u % 2], soft[:, u % 2], ACT.Ln, bias=1.0).then_inc(s_ln, 1)

            def sigmoids(it, u):
                g = it * UNROLL + u
                act.wait_ge(s_soft, 2 * g + 1)
                nc.scalar.activation(soft[:, u % 2, :, 0:C], soft[:, u % 2, :, 0:C], ACT.Exp).then_inc(s_sig, 1)

            def iteration(it):
                for u in range(UNROLL + 1):
                    if u < UNROLL:
                        copy_t(it, u)
                    if u >= 1:
                        logs(it, u - 1)
                        sigmoids(it, u - 1)
            iteration(0)
            with act.Fori(1, ITERS) as it:
                iteration(it)

        @block.tensor
        def _(pe):
            def transposes(it, u):
                g = it * UNROLL + u
                pe.wait_ge(s_S, g + 1)
                wait(pe, s_Tc, g - 1)
                for i in range(GROUP):
                    last = nc.tensor.transpose(k.psum[u % 2][:, i * P:(i + 1) * P], k.onehot[:, u, i, :], k.ident[:, :])
                last.then_inc(s_T, 1)

            def spread(it, u):
                g = it * UNROLL + u
                blocks = load_blocks(k, pe, it * ITER + u * GROUP)
                pe.wait_ge(s_Tc, g + 1)
                wait(pe, s_pre, g - 1)
                for i in range(GROUP):
                    last = nc.tensor.matmul(k.psum[2 + u % 2][:, i * P:(i + 1) * P], k.onehot_t[:, u % 2, i, :],
                                            p_tab[:, ds(blocks[i] * (2 * C), 2 * C)], start=True, stop=True)
                last.then_inc(s_X, 1)

            def segment_sum(it, u):
                g = it * UNROLL + u
                pe.wait_ge(s_msg, g + 1)
                if layer == 0:
                    pe.wait_ge(s_sig, g + 1)
                wait(pe, s_acc, (g - 1) * GROUP)
                for i in range(GROUP):
                    last = nc.tensor.matmul(k.psum[4 + u % 2][:, i * P:i * P + width], k.onehot[:, u, i, :],
                                            k.msg[:, u, i, 0:width], start=True, stop=True)
                last.then_inc(s_agg, 1)

            def iteration(it):
                for u in range(UNROLL + 3):
                    if u < UNROLL:
                        transposes(it, u)
                    if 0 <= u - 1 < UNROLL:
                        spread(it, u - 1)
                    if 0 <= u - 3 < UNROLL:
                        segment_sum(it, u - 3)
            if layer == 0:
                pe.wait_ge(s_zero, 2)
            iteration(0)
            with pe.Fori(1, ITERS) as it:
                iteration(it)


def layer_norm(nc, k, v, link, sq, s_act_in, s_act_out, n):
    mean, var = k.node_col[:, 0, :], k.node_col[:, 1, :]
    link(nc.vector.tensor_reduce(mean, k.node_a, AX.X, ALU.add))
    link(nc.vector.tensor_scalar(mean, mean, 1.0 / C, None, ALU.mult))
    nc.vector.tensor_tensor(k.node_a, k.node_a, mean.unsqueeze(2).broadcast_to([P, NB, C]), ALU.subtract).then_inc(s_act_in, 1)
    v.wait_ge(s_act_out, n + 1)
    link(nc.vector.tensor_reduce(var, sq, AX.X, ALU.add))
    nc.vector.tensor_scalar(var, var, 1.0 / C, EPS, ALU.mult, ALU.add).then_inc(s_act_in, 1)
    v.wait_ge(s_act_out, n + 2)
    link(nc.vector.reciprocal(var, var))
    link(nc.vector.tensor_tensor(k.node_a, k.node_a, var.unsqueeze(2).broadcast_to([P, NB, C]), ALU.mult))


def layer_norm_act(nc, k, act, sq, s_act_in, s_act_out, n):
    act.wait_ge(s_act_in, n + 1)
    nc.scalar.activation(sq, k.node_a, ACT.Square).then_inc(s_act_out, 1)
    act.wait_ge(s_act_in, n + 2)
    nc.scalar.activation(k.node_col[:, 1, :], k.node_col[:, 1, :], ACT.Sqrt).then_inc(s_act_out, 1)


def cg_finish(k, layer, x):
    nc = k.nc
    k.next_stage()
    n = f"cgf{layer}_"
    s_x, s_ch, s_in, s_out, s_st = (k.sem(n + c) for c in ("x", "chain", "act_in", "act_out", "store"))
    sq = k.big[:, 0:NB * C].rearrange("p (b c) -> p b c", c=C)
    with nc.Block() as block:
        @block.vector
        def _(v):
            link = Chain(v, s_ch)
            if layer == 0:
                nc.vector.tensor_copy(k.loop_sum[:, :, :], k.acc[:, :, C:AW])
            link(nc.vector.tensor_tensor(k.node_a, k.node_a, k.acc[:, :, 0:C], ALU.add))
            if layer == 0:
                link(nc.vector.tensor_scalar(k.node_a, k.node_a, 0.0, None, ALU.max))
                return
            nc.vector.memset(k.node_b[:, NB - 1, :], 0.0).then_inc(s_in, 1)
            v.wait_ge(s_x, 32)
            link(nc.vector.tensor_scalar(k.node_a, k.node_a, 0.0, None, ALU.max))
            link(nc.vector.tensor_tensor(k.node_a, k.node_a, k.node_b, ALU.add))
            layer_norm(nc, k, v, link, sq, s_in, s_out, 0)

        if layer == 1:
            @block.scalar
            def _(act):
                layer_norm_act(nc, k, act, sq, s_in, s_out, 0 + 1 - 0)

            @block.sync
            def _(sp):
                sp.wait_ge(s_in, 1)
                load_nodes(sp, k.node_b, x, s_x)
                sp.wait_ge(s_ch, CG_LN_LINKS)
                sp.dma_start(k.x1_dram.rearrange("(b p) c -> p b c", p=P), k.node_a).then_inc(s_st, 16)
                sp.wait_ge(s_st, 16)


CG_LN_LINKS = 8


def gat_tables(k, layer):
    nc = k.nc
    k.next_stage()
    n = f"gat{layer}_t_"
    s_z, s_h, s_t, s_tc, s_m, s_p, s_q, s_st, s_ch = (k.sem(n + x) for x in ("zero", "h", "t", "tc", "m", "p", "q", "store", "chain"))
    stage = k.big[:, 0:NB * TW].rearrange("p (b c) -> p b c", c=TW)
    rows = k.xl_table.rearrange("(b p) c -> p b c", p=P)
    a_src, a_dst, tmp, mean = (k.node_col[:, i, :] for i in range(4))

    h_stage = k.work[:, 0:2 * P].rearrange("p (j c) -> p j c", c=P)

    with nc.Block() as block:
        @block.gpsimd
        def _(pool):
            def body(b, j):
                wait(pool, s_t, b - 1)
                nc.gpsimd.tensor_copy(h_stage[:, j, 0:C], flat(k.node_a[:, ds(b, 1), :])).then_inc(s_h, 1)
            nc.gpsimd.memset(k.work[:, 0:2 * P], 0.0).then_inc(s_z, 1)
            pool.wait_ge(s_z, 1)
            body(0, 0)
            body(1, 1)
            with pool.Fori(1, NB // 2) as i:
                body(i * 2, 0)
                body(i * 2 + 1, 1)

        @block.tensor
        def _(pe):
            def body(b, j):
                pe.wait_ge(s_h, b + 1)
                wait(pe, s_tc, b - 1)
                nc.tensor.transpose(k.psum[j][:, 0:P], h_stage[:, j, :], k.ident[:, :]).then_inc(s_t, 1)
                pe.wait_ge(s_tc, b + 1)
                wait(pe, s_p, b - 1)
                wait(pe, s_q, b - 1)
                nc.tensor.matmul(k.psum[2 + j][:, 0:C + 2], k.xt[0:C, j, :], k.gw[:, layer, :], start=True, stop=True).then_inc(s_m, 1)
            body(0, 0)
            body(1, 1)
            with pe.Fori(1, NB // 2) as i:
                body(i * 2, 0)
                body(i * 2 + 1, 1)

        @block.scalar
        def _(act):
            def body(b, j):
                act.wait_ge(s_t, b + 1)
                wait(act, s_m, b - 1)
                nc.scalar.activation(k.xt[0:C, j, :], k.psum[j][0:C, 0:P], ACT.Copy).then_inc(s_tc, 1)
                act.wait_ge(s_m, b + 1)
                nc.scalar.activation(flat(stage[:, ds(b, 1), :]), k.psum[2 + j][:, 0:TW], ACT.Copy).then_inc(s_p, 1)
            body(0, 0)
            body(1, 1)
            with act.Fori(1, NB // 2) as i:
                body(i * 2, 0)
                body(i * 2 + 1, 1)

        @block.vector
        def _(v):
            def body(b, j):
                v.wait_ge(s_p, b + 1)
                nc.vector.tensor_copy(flat(k.node_b[:, ds(b, 1), :]), k.psum[2 + j][:, 0:C])
                nc.vector.tensor_copy(k.spread[:, ds(b, 1), 0:1], k.psum[2 + j][:, C + 1:C + 2].unsqueeze(2)).then_inc(s_q, 1)
            with v.Fori(0, NB // 2) as i:
                body(i * 2, 0)
                body(i * 2 + 1, 1)
            link = Chain(v, s_ch)
            v.wait_ge(s_q, NB)
            link(nc.vector.tensor_tensor(a_src, stage[:, :, C], k.spread[:, :, 0], ALU.add))
            link(nc.vector.tensor_scalar(tmp, k.loop_sum[:, :, 2], 1.0, None, ALU.max))
            link(nc.vector.reciprocal(tmp, tmp))
            link(nc.vector.tensor_tensor(mean, k.loop_sum[:, :, layer], tmp, ALU.mult))
            link(nc.vector.tensor_tensor(a_src, a_src, mean, ALU.add))
            link(nc.vector.scalar_tensor_tensor(k.spread[:, :, 1], a_src, SLOPE, a_src, ALU.mult, ALU.max))

        @block.sync
        def _(sp):
            k.clear_old(sp)
            with sp.Fori(0, NB // 14) as i:
                sp.wait_ge(s_p, i * 14 + 14)
                sp.dma_start(rows[:, ds(i * 14, 14), :], stage[:, ds(i * 14, 14), :]).then_inc(s_st, 16)
            sp.wait_ge(s_st, 16 * (NB // 14))


def gat_edges(k, layer):
    nc = k.nc
    k.next_stage()
    n = f"gat{layer}_e_"
    (s_zero, a_S, a_T, a_Tc, a_X, s_sc, s_x3, s_x3c, s_cc, s_cr, s_tu, s_tub, s_dif, s_exp, s_w, s_wt, s_wsw,
     s_fb, s_fv, s_fe, s_done, e_S, e_m, e_p, e_agg, e_acc, s_ch, s_idx) = (
        k.sem(n + x) for x in (
            "zero", "a_onehot", "a_trans", "a_trans_sb", "a_spread", "scores", "scores_t", "scores_t_sb", "cols", "rows",
            "carry", "carry_t", "diff", "exp", "weights", "weights_t", "weights_sb", "factor_ps", "factor_log", "factor",
            "rescaled", "e_onehot", "e_msg", "e_pair", "e_agg", "e_acc", "chain", "idx"))
    s_gat, gat_base = [k.rows[0:2], k.rows[2:4]], [k.row_base[0:2], k.row_base[2:4]]
    turns = [(NBATCH + 1) // 2, NBATCH // 2]
    k.row_base = [r + turns[i // 2] * HALF * 16 for i, r in enumerate(k.row_base)]
    s_turn = k.sem(n + "turn")
    buf = [k.big[:, i * P * TW:(i + 1) * P * TW].rearrange("p (s c) -> p s c", c=TW) for i in range(2)]
    w = k.work
    x3 = w[:, 0:3 * P].rearrange("p (j s) -> p j s", s=P)
    x3t = w[:, 3 * P:6 * P].rearrange("p (j e) -> p j e", e=P)
    valid, vneg = w[:, 6 * P:7 * P], w[:, 7 * P:8 * P]
    neq = w[:, 8 * P:9 * P + 1]
    pen = w[:, 9 * P + 8:10 * P + 9]
    fwd = w[:, 11 * P:12 * P]
    seg = w[:, 12 * P:13 * P]
    far = w[:, 13 * P:14 * P]
    wx = w[:, 14 * P:16 * P].rearrange("p (j e) -> p j e", e=P)
    wsw = w[:, 16 * P:18 * P].rearrange("p (s j) -> p s j", j=2)
    cols = w[:, 18 * P:18 * P + 4]
    carry = w[:, 18 * P + 4:18 * P + 6]
    fac = w[:, 18 * P + 6:18 * P + 7]
    single = w[:, 18 * P + 7:18 * P + 8]
    fpair = w[0:1, 18 * P + 8:18 * P + 10]
    at = 2 * P * TW
    t_row = k.big[0:1, at:at + P + 1]
    u_row = k.big[0:1, at + 136:at + 136 + P + 1]
    crow = k.big[0:1, at + 272:at + 272 + 4 * P]
    bank_ad = k.psum[2][:, 0:2 * P].rearrange("p (s j) -> p s j", j=2)
    LINKS = 26
    BIT = BGROUPS // UNROLL
    OUTER = (NBATCH - 1) // 2

    def over_batches(eng, batch):
        batch(0, 0, 0)
        with eng.Fori(0, OUTER) as j:
            batch(j * 2 + 1, 1, j)
            batch(j * 2 + 2, 0, j + 1)

    def over_groups(eng, b, body):
        if isinstance(b, int):
            body(0)
            with eng.Fori(1, BIT) as it:
                body(it)
        else:
            with eng.Fori(0, BIT) as it:
                body(it)

    with nc.Block() as block:
        @block.sync
        def _(sp):
            k.clear_old(sp)

        @block.gpsimd
        def _(pool):
            def batch(b, p, turn):
                wait(pool, e_m, (b - 1) * BGROUPS)
                for s in range(P):
                    half = s // HALF
                    if s == HALF // 2:
                        if p == 1 or not isinstance(b, int) or b:
                            pool.wait_ge(s_gat[1 - p][1], turn * (16 * HALF) + (p * 16 * HALF + gat_base[1 - p][1]))
                            pool.sem_inc(s_turn, 1)
                        nc.gpsimd.tensor_copy(k.idx_stage[:, HALF:P], k.src_idx[:, ds(b * P + HALF, HALF)]).then_inc(s_idx, 1)
                    if s == HALF + HALF // 2:
                        pool.wait_ge(s_gat[p][0], turn * (16 * HALF) + (16 * HALF + gat_base[p][0]))
                        pool.sem_inc(s_turn, 1)
                        nc.gpsimd.tensor_copy(k.idx_stage[:, 0:HALF], k.src_idx[:, ds(b * P + P, HALF)]).then_inc(s_idx, 1)
                    if s % HALF == 0:
                        pool.wait_ge(s_idx, b * 2 + half + 1)
                        pool.sem_inc(s_turn, 1)
                    pool.indirect_dma_start(out=buf[p][:, s, :], out_offset=None, in_=k.xl_table,
                                            in_offset=bass.IndirectOffsetOnAxis(ap=k.idx_stage[:, s:s + 1], axis=0)).then_inc(s_gat[p][half], 16)
            nc.gpsimd.tensor_copy(k.idx_stage[:, 0:HALF], k.src_idx[:, 0:HALF]).then_inc(s_idx, 1)
            batch(0, 0, 0)
            batch(1, 1, 0)
            with pool.Fori(1, OUTER) as j:
                batch(j * 2, 0, j)
                batch(j * 2 + 1, 1, j)
            batch(NBATCH - 1, 0, OUTER)

        @block.vector
        def _(v):
            nc.vector.memset(k.acc, 0.0).then_inc(s_zero, 1)
            nc.vector.memset(t_row[:, P:P + 1], BIG_NEG).then_inc(s_zero, 1)
            nc.vector.memset(u_row[:, P:P + 1], BIG_NEG).then_inc(s_zero, 1)
            v.wait_ge(s_zero, 3)

            def batch(b, p, turn):
                first_group = b * BGROUPS
                gather = buf[p]

                def spread(it):
                    for u in range(UNROLL):
                        g = first_group + it * UNROLL + u
                        wait(v, a_T, g - 3)
                        build_onehot(k, nc, u, (b * BIT + it) * ITER + u * GROUP).then_inc(a_S, 1)
                over_groups(v, b, spread)

                link = Chain(v, s_ch, b * LINKS)
                key = k.keys[:, ds(b * (P + 2), P + 2)]
                rel = k.dst_rel[:, ds(b * P, P)]
                link(nc.vector.tensor_scalar(valid, rel, 0.0, None, ALU.is_ge))
                link(nc.vector.scalar_tensor_tensor(valid, rel, float(P), valid, ALU.is_lt, ALU.mult))
                link(nc.vector.tensor_scalar(vneg, valid, 1.0, -BIG_NEG, ALU.subtract, ALU.mult))
                link(nc.vector.tensor_tensor(neq, key[:, 1:P + 2], key[:, 0:P + 1], ALU.not_equal))
                link(nc.vector.tensor_scalar(pen, neq, BIG_NEG, None, ALU.mult))
                link(nc.vector.tensor_tensor(single, key[:, 1:2], key[:, P:P + 1], ALU.not_equal))
                link(nc.vector.tensor_scalar(single, single, BIG_NEG, None, ALU.mult))
                link(nc.vector.tensor_tensor(cols[:, 0:1], pen[:, 0:1], single, ALU.add))
                link(nc.vector.tensor_tensor(cols[:, 3:4], pen[:, P:P + 1], single, ALU.add))
                link(nc.vector.tensor_copy(t_row[:, 0:1], t_row[:, P:P + 1]))
                v.wait_ge(a_X, first_group + BGROUPS)
                for half in range(2):
                    v.wait_ge(s_gat[p][half], turn * (16 * HALF) + (16 * HALF + gat_base[p][half]))
                link(nc.vector.tensor_tensor(x3[:, 0, :], gather[:, :, C], bank_ad[:, :, 0], ALU.add))
                link(nc.vector.tensor_tensor(x3[:, 0, :], x3[:, 0, :], k.ae[:, ds(b * P, P), layer], ALU.add))
                link(nc.vector.scalar_tensor_tensor(x3[:, 0, :], x3[:, 0, :], SLOPE, x3[:, 0, :], ALU.mult, ALU.max))
                nc.vector.tensor_copy(x3[:, 2, :], bank_ad[:, :, 1])
                link(nc.vector.tensor_tensor(x3[:, 1, :], x3[:, 0, :], bank_ad[:, :, 1], ALU.max))
                link(nc.vector.tensor_tensor(x3, x3, valid.unsqueeze(1).broadcast_to([P, 3, P]), ALU.mult))
                nc.vector.tensor_tensor(x3, x3, vneg.unsqueeze(1).broadcast_to([P, 3, P]), ALU.add).then_inc(s_sc, 1)
                v.wait_ge(s_x3c, b + 1)
                link(nc.vector.tensor_tensor_scan(fwd, pen[:, 0:P], x3t[:, 1, :], BIG_NEG, ALU.add, ALU.max))
                link(nc.vector.tensor_tensor_scan(seg[:, ::-1], pen[:, 1:P + 1][:, ::-1], fwd[:, ::-1], BIG_NEG, ALU.add, ALU.max))
                nc.vector.tensor_copy(cols[:, 1:2], seg[:, P - 1:P]).then_inc(s_cc, 1)
                nc.vector.tensor_copy(cols[:, 2:3], seg[:, 0:1]).then_inc(s_cc, 1)
                v.wait_ge(s_cr, b + 1)
                link(nc.vector.tensor_copy(crow, k.psum[4][0:1, :]))
                nc.vector.tensor_tensor_scan(t_row[:, 1:P + 1], crow[:, 0:P], crow[:, P:2 * P], t_row[:, 0:1], ALU.add, ALU.max).then_inc(s_tu, 1)
                nc.vector.tensor_tensor_scan(u_row[:, 0:P][:, ::-1], crow[:, 3 * P:4 * P][:, ::-1], crow[:, 2 * P:3 * P][:, ::-1],
                                             BIG_NEG, ALU.add, ALU.max).then_inc(s_tu, 1)
                v.wait_ge(s_tub, b + 1)
                link(nc.vector.tensor_tensor(carry[:, 0:1], k.psum[5][:, 0:1], pen[:, 0:1], ALU.add))
                link(nc.vector.tensor_tensor(carry[:, 1:2], k.psum[5][:, 1:2], pen[:, P:P + 1], ALU.add))
                for side, edge in ((0, 1), (1, P)):
                    link(nc.vector.tensor_scalar(far, key[:, 1:P + 1], key[:, edge:edge + 1], BIG_NEG, ALU.not_equal, ALU.mult))
                    link(nc.vector.scalar_tensor_tensor(seg, far, carry[:, side:side + 1], seg, ALU.add, ALU.max))
                nc.vector.tensor_tensor(wx[:, 0, :], x3t[:, 0, :], seg, ALU.subtract).then_inc(s_dif, 1)
                nc.vector.tensor_tensor(wx[:, 1, :], x3t[:, 2, :], seg, ALU.subtract).then_inc(s_dif, 1)
                link(nc.vector.tensor_tensor(fpair[:, 0:1], t_row[:, 0:1], seg[0:1, 0:1], ALU.subtract))
                link(nc.vector.tensor_scalar(neq[0:1, 0:1], neq[0:1, 0:1], -1.0, 1.0, ALU.mult, ALU.add))
                nc.vector.tensor_tensor(fpair[:, 0:1], fpair[:, 0:1], neq[0:1, 0:1], ALU.mult).then_inc(s_fb, 1)
                nc.vector.tensor_copy(fpair[:, 1:2], rel[0:1, 0:1]).then_inc(s_fb, 1)
                v.wait_ge(s_exp, b + 1)
                nc.vector.tensor_tensor(wx[:, 1, :], wx[:, 1, :], neq[:, 1:P + 1], ALU.mult).then_inc(s_w, 1)
                v.wait_ge(s_fv, b + 1)
                nc.vector.tensor_scalar(fac, k.iota_col[:, :], k.psum[5][:, 9:10], k.psum[5][:, 8:9], ALU.is_equal, ALU.mult).then_inc(s_fe, 1)
                blk = v.value_load(k.block_row[0:1, ds(b * P, 1)], min_val=0, max_val=NB - 1)
                v.wait_ge(s_fe, 2 * b + 2)
                wait(v, e_acc, first_group * GROUP)
                to = flat(k.acc[:, ds(blk, 1), 0:C + 1])
                nc.vector.tensor_scalar(to, to, fac, None, ALU.mult).then_inc(s_done, 1)

                def sums(it):
                    def weigh(u):
                        g = first_group + it * UNROLL + u
                        wait(v, e_agg, g - 3)
                        build_onehot(k, nc, u, (b * BIT + it) * ITER + u * GROUP).then_inc(e_S, 1)
                        s = it * ITER + u * GROUP
                        v.wait_ge(s_wsw, b + 1)
                        nc.vector.tensor_tensor(k.msg[:, u, :, 0:C], gather[:, ds(s, GROUP), 0:C],
                                                wsw[:, ds(s, GROUP), 0:1].broadcast_to([P, GROUP, C]), ALU.mult).then_inc(e_m, 1)

                    def accumulate(u):
                        g = first_group + it * UNROLL + u
                        blocks = load_blocks(k, v, (b * BIT + it) * ITER + u * GROUP)
                        v.wait_ge(e_agg, g + 1)
                        v.wait_ge(s_done, b + 1)
                        for i in range(GROUP):
                            wait(v, e_acc, g * GROUP + i)
                            to = flat(k.acc[:, ds(blocks[i], 1), 0:C + 2])
                            nc.vector.tensor_tensor(to, to, k.psum[6 + u % 2][:, i * P:i * P + C + 2], ALU.add).then_inc(e_acc, 1)
                    for u in range(UNROLL + 1):
                        if u < UNROLL:
                            weigh(u)
                        if u:
                            accumulate(u - 1)
                over_groups(v, b, sums)
                assert link.n == LINKS, link.n
            over_batches(v, batch)

        @block.scalar
        def _(act):
            act.preload_act_table_set("natural_log_exp_and_others")

            def batch(b, p, turn):
                first_group = b * BGROUPS

                def spread(it):
                    for u in range(UNROLL):
                        g = first_group + it * UNROLL + u
                        act.wait_ge(a_T, g + 1)
                        wait(act, a_X, g - 1)
                        nc.scalar.activation(k.onehot_t[:, u % 2, :, :], k.psum[u % 2][:, :].rearrange("p (i c) -> p i c", c=P), ACT.Copy).then_inc(a_Tc, 1)
                over_groups(act, b, spread)
                act.wait_ge(s_x3, b + 1)
                nc.scalar.activation(x3t, k.psum[3][:, 0:3 * P].rearrange("p (j e) -> p j e", e=P), ACT.Copy).then_inc(s_x3c, 1)
                act.wait_ge(s_dif, 2 * b + 2)
                nc.scalar.activation(wx, wx, ACT.Exp).then_inc(s_exp, 1)
                act.wait_ge(s_fe, 2 * b + 1)
                nc.scalar.activation(fac, fac, ACT.Exp).then_inc(s_fe, 1)
                act.wait_ge(s_wt, b + 1)
                nc.scalar.activation(wsw.rearrange("p s j -> p j s"), k.psum[3][:, 0:2 * P].rearrange("p (j s) -> p j s", s=P), ACT.Copy).then_inc(s_wsw, 1)
                act.wait_ge(s_wsw, b + 1)

                def sums(it):
                    for u in range(UNROLL):
                        g = first_group + it * UNROLL + u
                        wait(act, e_agg, g - 3)
                        nc.scalar.activation(k.msg[:, u, :, C:C + 2], wsw[:, ds(it * ITER + u * GROUP, GROUP), :], ACT.Copy).then_inc(e_p, 1)
                over_groups(act, b, sums)
            over_batches(act, batch)

        @block.tensor
        def _(pe):
            def batch(b, p, turn):
                first_group = b * BGROUPS

                def spread(it):
                    def transposes(u):
                        g = first_group + it * UNROLL + u
                        pe.wait_ge(a_S, g + 1)
                        wait(pe, a_Tc, g - 1)
                        for i in range(GROUP):
                            last = nc.tensor.transpose(k.psum[u % 2][:, i * P:(i + 1) * P], k.onehot[:, u, i, :], k.ident[:, :])
                        last.then_inc(a_T, 1)

                    def expand(u):
                        g = first_group + it * UNROLL + u
                        blocks = load_blocks(k, pe, (b * BIT + it) * ITER + u * GROUP)
                        pe.wait_ge(a_Tc, g + 1)
                        wait(pe, s_sc, b)
                        for i in range(GROUP):
                            last = nc.tensor.matmul(k.psum[2][:, ds((it * ITER + u * GROUP + i) * 2, 2)], k.onehot_t[:, u % 2, i, :],
                                                    flat(k.spread[:, ds(blocks[i], 1), :]), start=True, stop=True)
                        last.then_inc(a_X, 1)
                    for u in range(UNROLL + 1):
                        if u < UNROLL:
                            transposes(u)
                        if u:
                            expand(u - 1)
                over_groups(pe, b, spread)
                pe.wait_ge(s_sc, b + 1)
                for j in range(3):
                    last = nc.tensor.transpose(k.psum[3][:, j * P:(j + 1) * P], x3[:, j, :], k.ident[:, :])
                last.then_inc(s_x3, 1)
                pe.wait_ge(s_cc, 2 * b + 2)
                for j in range(4):
                    last = nc.tensor.transpose(k.psum[4][0:1, j * P:(j + 1) * P], cols[:, j:j + 1], k.ident[:, :])
                last.then_inc(s_cr, 1)
                pe.wait_ge(s_tu, 2 * b + 2)
                nc.tensor.matmul(k.psum[5][:, 0:1], t_row[:, 0:P], k.ones_row[:, 0:1], start=True, stop=True)
                nc.tensor.matmul(k.psum[5][:, 1:2], u_row[:, 1:P + 1], k.ones_row[:, 0:1], start=True, stop=True).then_inc(s_tub, 1)
                pe.wait_ge(s_fb, 2 * b + 2)
                nc.tensor.matmul(k.psum[5][:, 8:10], k.ones_row[:, :], fpair, start=True, stop=True).then_inc(s_fv, 1)
                pe.wait_ge(s_w, b + 1)
                for j in range(2):
                    last = nc.tensor.transpose(k.psum[3][:, j * P:(j + 1) * P], wx[:, j, :], k.ident[:, :])
                last.then_inc(s_wt, 1)

                def sums(it):
                    for u in range(UNROLL):
                        g = first_group + it * UNROLL + u
                        pe.wait_ge(e_m, g + 1)
                        pe.wait_ge(e_p, g + 1)
                        wait(pe, e_acc, (g - 1) * GROUP)
                        for i in range(GROUP):
                            last = nc.tensor.matmul(k.psum[6 + u % 2][:, i * P:i * P + C + 2], k.onehot[:, u, i, :],
                                                    k.msg[:, u, i, 0:C + 2], start=True, stop=True)
                        last.then_inc(e_agg, 1)
                over_groups(pe, b, sums)
            over_batches(pe, batch)


def gat_finish(k, layer, out):
    nc = k.nc
    k.next_stage()
    n = f"gat{layer}_f_"
    s_ch, s_in, s_aout, s_mm, s_x, s_st = (k.sem(n + x) for x in ("chain", "act_in", "act_out", "colsum", "x1", "store"))
    sq = k.big[:, 0:NB * C].rearrange("p (b c) -> p b c", c=C)
    selfw, den = k.node_col[:, 0, :], k.node_col[:, 1, :]
    psums = k.work[:, 0:C]
    mean = k.work[:, C:2 * C]
    std = k.work[:, 2 * C:3 * C]
    bias, gamma, beta = (k.gvec[:, 3 * layer + j, :] for j in range(3))
    a = k.node_a

    def over_nodes(vec):
        return vec.unsqueeze(1).broadcast_to([P, NB, C])

    def over_chan(vec):
        return vec.unsqueeze(2).broadcast_to([P, NB, C])

    with nc.Block() as block:
        @block.vector
        def _(v):
            link = Chain(v, s_ch)
            link(nc.vector.tensor_scalar(selfw, k.loop_sum[:, :, 2], 0.0, None, ALU.is_equal))
            link(nc.vector.tensor_tensor(selfw, selfw, k.acc[:, :, C + 1], ALU.add))
            link(nc.vector.tensor_tensor(den, selfw, k.acc[:, :, C], ALU.add))
            link(nc.vector.reciprocal(den, den))
            link(nc.vector.tensor_tensor(a, k.node_b, over_chan(selfw), ALU.mult))
            link(nc.vector.tensor_tensor(a, a, k.acc[:, :, 0:C], ALU.add))
            link(nc.vector.tensor_tensor(a, a, over_chan(den), ALU.mult))
            link(nc.vector.tensor_tensor(a, a, over_nodes(bias), ALU.add))
            link(nc.vector.tensor_scalar(a[:, NB - 1, :], a[:, NB - 1, :], k.row_mask[:, :], None, ALU.mult))
            nc.vector.tensor_reduce(psums, a.rearrange("p b c -> p c b"), AX.X, ALU.add).then_inc(s_in, 1)
            v.wait_ge(s_mm, 1)
            link(nc.vector.tensor_scalar(mean, k.psum[0][:, 0:C], 1.0 / N, None, ALU.mult))
            link(nc.vector.tensor_tensor(a, a, over_nodes(mean), ALU.subtract))
            nc.vector.tensor_scalar(a[:, NB - 1, :], a[:, NB - 1, :], k.row_mask[:, :], None, ALU.mult).then_inc(s_in, 1)
            v.wait_ge(s_aout, 1)
            nc.vector.tensor_reduce(psums, sq.rearrange("p b c -> p c b"), AX.X, ALU.add).then_inc(s_in, 1)
            v.wait_ge(s_mm, 2)
            nc.vector.tensor_scalar(std, k.psum[0][:, C:2 * C], 1.0 / N, EPS, ALU.mult, ALU.add).then_inc(s_in, 1)
            v.wait_ge(s_aout, 2)
            link(nc.vector.reciprocal(std, std))
            link(nc.vector.tensor_tensor(std, std, gamma, ALU.mult))
            link(nc.vector.tensor_tensor(a, a, over_nodes(std), ALU.mult))
            link(nc.vector.tensor_tensor(a, a, over_nodes(beta), ALU.add))
            if layer == 0:
                link(nc.vector.tensor_scalar(a, a, 0.0, None, ALU.max))
                return
            v.wait_ge(s_x, 16)
            link(nc.vector.tensor_tensor(a, a, k.node_b, ALU.add))
            layer_norm(nc, k, v, link, sq, s_in, s_aout, 2)

        @block.tensor
        def _(pe):
            pe.wait_ge(s_in, 1)
            nc.tensor.matmul(k.psum[0][:, 0:C], k.ones_sq[:, :], psums, start=True, stop=True).then_inc(s_mm, 1)
            pe.wait_ge(s_in, 3)
            nc.tensor.matmul(k.psum[0][:, C:2 * C], k.ones_sq[:, :], psums, start=True, stop=True).then_inc(s_mm, 1)

        @block.scalar
        def _(act):
            act.wait_ge(s_in, 2)
            nc.scalar.activation(sq, a, ACT.Square).then_inc(s_aout, 1)
            act.wait_ge(s_in, 4)
            nc.scalar.activation(std, std, ACT.Sqrt).then_inc(s_aout, 1)
            if layer == 1:
                layer_norm_act(nc, k, act, sq, s_in, s_aout, 4)

        @block.sync
        def _(sp):
            k.clear_old(sp)
            if layer == 1:
                sp.wait_ge(s_ch, 5)
                sp.dma_start(k.node_b, k.x1_dram.rearrange("(b p) c -> p b c", p=P)).then_inc(s_x, 16)
                sp.wait_ge(s_ch, GAT_LINKS)
                full = (NB - 1) * P
                sp.dma_start(out[0:full, :].rearrange("(b p) c -> p b c", p=P), k.node_a[:, 0:NB - 1, :]).then_inc(s_st, 16)
                sp.dma_start(out[full:N, :], k.node_a[0:LAST, NB - 1, :]).then_inc(s_st, 16)
                sp.wait_ge(s_st, 32)


GAT_LINKS = 21


def gnn_resnorm_kernel(nc, a, out, upto=99):
    ctx = ExitStack()
    with ctx:
        k = Core(nc, ctx)
        setup(k, a)
        for layer in range(2):
            cg_tables(k, layer)
            cg_edges(k, layer)
            cg_finish(k, layer, a["x"])
        for layer in range(2):
            gat_tables(k, layer)
            gat_edges(k, layer)
            gat_finish(k, layer, out)
        k.close()


_INS = ["x", "src", "dst", "edge_attr_16",
        "L0_gnn_Wf1", "L0_gnn_bf1", "L0_gnn_Ws1", "L0_gnn_bs1", "L0_gnn_Wf2", "L0_gnn_bf2", "L0_gnn_Ws2", "L0_gnn_bs2",
        "L1_gnn_W0", "L1_gnn_We0", "L1_gnn_as0", "L1_gnn_ad0", "L1_gnn_ae0", "L1_gnn_b0", "L1_gnn_g0", "L1_gnn_beta0",
        "L1_gnn_W1", "L1_gnn_We1", "L1_gnn_as1", "L1_gnn_ad1", "L1_gnn_ae1", "L1_gnn_b1", "L1_gnn_gf", "L1_gnn_betaf"]


def kernel(**inputs):
    import numpy as np
    import concourse.bacc as bacc
    from concourse.bass_utils import run_bass_kernel_spmd as run

    nc = bacc.Bacc("TRN2", target_bir_lowering=False, num_devices=1)
    arrays, aps = {}, {}
    for name in _INS:
        arr = np.ascontiguousarray(inputs[name])
        arrays["in_" + name] = arr
        aps[name] = nc.dram_tensor("in_" + name, arr.shape, mybir.dt.from_np(arr.dtype), kind="ExternalInput").ap()
    out = nc.dram_tensor("out_0", (N, C), F32, kind="ExternalOutput").ap()
    gnn_resnorm_kernel(nc, aps, out)
    r = run(nc, [arrays], core_ids=[0])
    return r.results[0]["out_0"]
```

```python
from contextlib import ExitStack

import concourse.bass as bass
from concourse import mybir
from concourse.alu_op_type import AluOpType as ALU

F32 = mybir.dt.float32
BF16 = mybir.dt.bfloat16
I32 = mybir.dt.int32
ACT = mybir.ActivationFunctionType
AX = mybir.AxisListType
ds = bass.ds

P = 128
N = 12500
E = 200000
C = 64
D = 16
NB = -(-N // P)
LAST = N - (NB - 1) * P
TILES = -(-E // P)
FULL = E // P
NBATCH = -(-(TILES + NB - 1) // P)
STEPS = NBATCH * P
GROUP = 4
UNROLL = 4
ITER = GROUP * UNROLL
GROUPS = STEPS // GROUP
BGROUPS = P // GROUP
CH = NBATCH
PAD = 32768.0
BIG_NEG = -1.0e30
AW = C + 3
TW = C + 1
ACC_ROW, TAB_ROW, SPREAD_ROW = 0, 32, 64
HALF = P // 2
RING = UNROLL * GROUP * 2 * C
BIG = NB * 2 * C + RING
PREV, KEY, NEXT, SRC, AE = 0, 1, 1 + P, 2 + P, 2 + 2 * P
RW = AE + 2 * P
SLOPE = 0.2
EPS = 1e-5


def wait(eng, sem, value):
    if isinstance(value, int) and value <= 0:
        return
    eng.wait_ge(sem, value)


def flat(ap):
    return ap.rearrange("p o c -> p (o c)")


class Core:

    def __init__(self, nc, ctx):
        self.nc, self.ctx = nc, ctx
        self.old, self.cur = None, (ExitStack(), [])
        self.setup_rows = [ctx.enter_context(nc.semaphore(f"setup_rows{i}")) for i in range(2)]
        self.rows = [ctx.enter_context(nc.semaphore(f"rows{i}")) for i in range(4)]
        self.row_base = [0] * 4

        def sb(name, shape, dt=F32):
            return ctx.enter_context(nc.sbuf_tensor(name, shape, dt))

        self.sb = sb
        self.big = sb("big", [P, BIG + NB * C])
        self.node_a = self.big[:, BIG:BIG + NB * C].rearrange("p (b c) -> p b c", c=C)
        self.wide = sb("wide", [P, NB * C + NB * AW])
        self.node_b = self.wide[:, 0:NB * C].rearrange("p (b c) -> p b c", c=C)
        self.acc = self.wide[:, NB * C:NB * (C + AW)].rearrange("p (b c) -> p b c", c=AW)
        self.src_idx = sb("src_idx", [P, STEPS + HALF], I32)
        self.dst_rel = sb("dst_rel", [P, STEPS])
        self.ae = sb("ae", [P, STEPS, 2])
        self.keys = sb("keys", [P, NBATCH * (P + 2)])
        self.offsets = sb("offsets", [65, STEPS], I32)
        self.idx_stage = sb("idx_stage", [P, P], I32)
        self.onehot = sb("onehot", [P, UNROLL, GROUP, P])
        self.onehot_t = sb("onehot_t", [P, 2, GROUP, P])
        self.msg = sb("msg", [P, UNROLL, GROUP, AW])
        self.work = sb("work", [P, 18 * P + 16])
        self.ident = sb("ident", [P, P])
        self.iota = sb("iota", [P, P])
        self.iota_col = sb("iota_col", [P, 1])
        self.ones_row = sb("ones_row", [1, P])
        self.ones_sq = sb("ones_sq", [P, P])
        self.row_mask = sb("row_mask", [P, 1])
        self.loop_sum = sb("loop_sum", [P, NB, 3])
        self.small = sb("small", [P, NB * 6])
        self.spread = self.small[:, 0:2 * NB].rearrange("p (b j) -> p b j", j=2)
        self.node_col = self.small[:, 2 * NB:6 * NB].rearrange("p (j b) -> p j b", b=NB)
        self.wc = self.small[0:C + 1, 0:8 * C].rearrange("p (l c) -> p l c", l=2)
        self.xt = sb("xt", [C + 1, 2, P])
        self.gw = sb("gw", [C, 2, C + 2])
        self.gvec = sb("gvec", [P, 6, C])
        self.psum = [ctx.enter_context(nc.psum_tensor(f"bank{i}", [P, 512], F32)) for i in range(8)]
        self.edge_rows = nc.dram_tensor("edge_rows", (NBATCH * P, RW), F32, kind="Internal").ap()
        self.q_table = nc.dram_tensor("q_table", (NB * P, 2 * C), F32, kind="Internal").ap()
        self.xl_table = nc.dram_tensor("xl_table", (NB * P, TW), F32, kind="Internal").ap()
        self.x1_dram = nc.dram_tensor("x1_dram", (NB * P, C), F32, kind="Internal").ap()

    def next_stage(self):
        if self.old is not None:
            self.old[0].close()
        self.old, self.cur = self.cur, (ExitStack(), [])

    def sem(self, name):
        handle = self.cur[0].enter_context(self.nc.semaphore(name))
        self.cur[1].append(handle)
        return handle

    def clear_old(self, sp):
        for handle in self.old[1]:
            sp.sem_clear(handle)

    def close(self):
        self.old[0].close()
        self.cur[0].close()


class Chain:

    def __init__(self, eng, sem, base=0):
        self.eng, self.sem, self.base, self.n = eng, sem, base, 0

    def __call__(self, ins):
        self.n += 1
        ins.then_inc(self.sem, 1)
        self.eng.wait_ge(self.sem, self.base + self.n)


def load_nodes(eng, dst, x, sem):
    full = (NB - 1) * P
    eng.dma_start(dst[:, 0:NB - 1, :], x[0:full, :].rearrange("(b p) c -> p b c", p=P)).then_inc(sem, 16)
    eng.dma_start(dst[0:LAST, NB - 1, :], x[full:N, :]).then_inc(sem, 16)


def setup(k, a):
    nc = k.nc
    k.next_stage()
    s_const, s_pad, s_int = k.sem("set_const"), k.sem("set_pad"), k.sem("set_int")
    s_w, s_x, s_ea = k.sem("set_weights"), k.sem("set_x"), [k.sem("set_ea0"), k.sem("set_ea1")]
    s_rows, s_thr, s_cmp, s_cnt = k.sem("set_rows"), k.sem("set_thr"), k.sem("set_cmp"), k.sem("set_cnt")
    s_trow, s_tcol, s_tidx = k.sem("set_trow"), k.sem("set_tcol"), k.sem("set_tidx")
    s_prod, s_red, s_store = k.sem("set_prod"), k.sem("set_red"), k.sem("set_store")
    s_g, s_rel, s_tr, s_out = k.setup_rows, k.sem("set_rel"), k.sem("set_tr"), k.sem("set_out")
    s_wt, s_wtc, s_wv, s_wvc = k.sem("set_wt"), k.sem("set_wtc"), k.sem("set_wv"), k.sem("set_wvc")
    s_ch = k.sem("set_chain")

    rows = k.big[:, 0:CH * RW].rearrange("p (c w) -> p c w", w=RW)
    at = CH * RW
    dint = k.big[:, at:at + CH * P].bitcast(I32).rearrange("p (c e) -> p c e", e=P)
    at += CH * P
    sint = k.big[:, at:at + CH * P].bitcast(I32).rearrange("p (c e) -> p c e", e=P)
    at += CH * P
    ea = [k.big[:, at + i * P * D:at + (i + 1) * P * D].rearrange("p (e d) -> p e d", d=D) for i in range(2)]
    prod = k.wide[:, 8000:8000 + P * D].rearrange("p (e d) -> p e d", d=D)
    neigh = k.work[:, 0:2 * CH].bitcast(I32).rearrange("p (c w) -> p c w", w=2)
    blk = k.work[:, 32:32 + CH].bitcast(I32)
    thr = k.work[:, 48:48 + CH]
    tile1 = k.work[:, 64:64 + CH]
    step_col = k.work[:, 80:80 + CH]
    tcol = k.work[:, 96:96 + CH]
    tidx = k.work[:, 112:112 + CH].bitcast(I32)
    off = k.work[:, 128:128 + CH]
    ones_bf = k.work[:, 144:145].bitcast(BF16)[:, 0:1]
    vb = k.work[:, 160:160 + 2 * D].rearrange("p (l d) -> p l d", d=D)
    wet = k.work[0:C, 192:192 + 2 * D].rearrange("p (l d) -> p l d", d=D)
    att = k.work[0:C, 224:230]
    aeb = k.work[0:C, 256:512].rearrange("p (l e) -> p l e", e=P)
    wt = k.work[0:C, 512:512 + 2 * C].rearrange("p (l c) -> p l c", c=C)
    we = k.work[0:D, 640:640 + 2 * C].rearrange("p (l c) -> p l c", c=C)
    t_row = k.wide[0:1, 0:STEPS]
    b_row = k.wide[0:1, STEPS:2 * STEPS]
    iota_s = k.wide[:, 2 * STEPS:3 * STEPS]
    cmp = [k.wide[:, 3 * STEPS + i * STEPS // 2:3 * STEPS + (i + 1) * STEPS // 2].bitcast(BF16) for i in range(2)]
    at = 4 * STEPS
    gath = [k.wide[:, at + i * RW:at + (i + 1) * RW] for i in range(2)]
    at += 2 * RW
    rel = [k.wide[:, at + i * P:at + (i + 1) * P] for i in range(2)]
    part = FULL - (CH - 1) * P
    tail = E - FULL * P
    NCONST, NRED = 12, 2

    with nc.Block() as block:
        @block.gpsimd
        def _(pool):
            nc.gpsimd.memset(rows[:, CH - 1, :], 0.0).then_inc(s_pad, 1)
            nc.gpsimd.memset(dint[:, CH - 1, :], int(PAD)).then_inc(s_pad, 1)
            nc.gpsimd.memset(sint[:, CH - 1, :], 0).then_inc(s_pad, 1)
            nc.gpsimd.memset(k.src_idx[:, STEPS:STEPS + HALF], 0)
            nc.gpsimd.memset(neigh, -1).then_inc(s_pad, 1)
            nc.gpsimd.memset(k.node_a[:, NB - 1, :], 0.0).then_inc(s_pad, 1)
            nc.gpsimd.iota(tile1, pattern=[[P, CH]], base=1, channel_multiplier=1, allow_small_or_imprecise_dtypes=True).then_inc(s_const, 1)
            nc.gpsimd.iota(iota_s, pattern=[[1, STEPS]], base=0, channel_multiplier=0, allow_small_or_imprecise_dtypes=True).then_inc(s_const, 1)
            nc.gpsimd.memset(ones_bf, 1.0).then_inc(s_const, 1)
            nc.gpsimd.memset(k.ident[:, :], 0.0).then_inc(s_const, 1)
            nc.gpsimd.memset(k.row_mask[:, :], 1.0).then_inc(s_const, 1)
            nc.gpsimd.iota(k.iota[:, :], pattern=[[1, P]], base=0, channel_multiplier=0, allow_small_or_imprecise_dtypes=True).then_inc(s_const, 1)
            nc.gpsimd.iota(k.iota_col[:, :], pattern=[[0, 1]], base=0, channel_multiplier=1, allow_small_or_imprecise_dtypes=True).then_inc(s_const, 1)
            nc.gpsimd.iota(step_col, pattern=[[P, CH]], base=0, channel_multiplier=1, allow_small_or_imprecise_dtypes=True).then_inc(s_const, 1)
            nc.gpsimd.memset(k.ones_row[:, :], 1.0).then_inc(s_const, 1)
            nc.gpsimd.memset(k.ones_sq[:, :], 1.0).then_inc(s_const, 1)
            pool.wait_ge(s_const, 10)
            nc.gpsimd.affine_select(out=k.ident[:, :], in_=k.ident[:, :], compare_op=ALU.not_equal, fill=1.0,
                                    base=0, pattern=[[-1, P]], channel_multiplier=1).then_inc(s_const, 1)
            nc.gpsimd.affine_select(out=k.row_mask[:, :], in_=k.row_mask[:, :], compare_op=ALU.is_ge, fill=0.0,
                                    base=LAST - 1, pattern=[[0, 1]], channel_multiplier=-1).then_inc(s_const, 1)
            pool.wait_ge(s_store, 16)
            pool.wait_ge(s_tidx, 1)
            for b in range(NBATCH):
                if b >= 2:
                    pool.wait_ge(s_rel, 2 * (b - 1))
                    pool.wait_ge(s_tr, b - 1)
                pool.indirect_dma_start(out=gath[b % 2], out_offset=None, in_=k.edge_rows,
                                        in_offset=bass.IndirectOffsetOnAxis(ap=tidx[:, b:b + 1], axis=0)).then_inc(s_g[b % 2], 16)

        @block.sync
        def _(sp):
            k.clear_old(sp)
            with nc.allow_non_contiguous_dma(reason="one neighbouring key per tile"):
                sp.wait_ge(s_pad, 7)
                head = (CH - 1) * P
                for src, dst in ((a["dst"], dint), (a["src"], sint)):
                    sp.dma_start(dst[:, 0:CH - 1, :], src[0:head * P].rearrange("(c p e) -> p c e", p=P, e=P)).then_inc(s_int, 16)
                    sp.dma_start(dst[0:part, CH - 1, :], src[head * P:FULL * P].rearrange("(p e) -> p e", e=P)).then_inc(s_int, 16)
                    sp.dma_start(dst[part:part + 1, CH - 1, 0:tail], src[FULL * P:E].rearrange("(p e) -> p e", p=1)).then_inc(s_int, 16)
                by_tile = a["dst"][0:FULL * P].rearrange("(t e) -> t e", e=P)
                for c in range(CH):
                    lo = 1 if c == 0 else 0
                    hi = P if c < CH - 1 else part + 1
                    sp.dma_start(neigh[lo:hi, c, 0:1], by_tile[c * P + lo - 1:c * P + hi - 1, P - 1:P]).then_inc(s_int, 16)
                    hi = P if c < CH - 1 else part - 1
                    sp.dma_start(neigh[0:hi, c, 1:2], by_tile[c * P + 1:c * P + 1 + hi, 0:1]).then_inc(s_int, 16)
                sp.dma_start(neigh[part - 1:part, CH - 1, 1:2], a["dst"][FULL * P:FULL * P + 1].rearrange("(p e) -> p e", p=1)).then_inc(s_int, 16)
            load_nodes(sp, k.node_a, a["x"], s_x)
            sp.wait_ge(s_rows, 1)
            sp.wait_ge(s_red, NRED * CH + 1)
            sp.dma_start(k.edge_rows.rearrange("(c p) w -> p c w", p=P), rows).then_inc(s_store, 16)
            sp.wait_ge(s_store, 16)
            sp.wait_ge(s_x, 32)

        @block.scalar
        def _(act):
            n = 0
            def w(out, in_):
                act.dma_start(out, in_).then_inc(s_w, 16)
            act.wait_ge(s_pad, 7)
            for l, we_n in enumerate(("L1_gnn_We0", "L1_gnn_We1")):
                w(we[:, l, :], a[we_n])
                w(k.gw[:, l, 0:C], a[f"L1_gnn_W{l}"])
                for j, v in enumerate(("as", "ad", "ae")):
                    w(att[:, 3 * l + j:3 * l + j + 1], a[f"L1_gnn_{v}{l}"].rearrange("a h c -> c (a h)"))
            for l in range(2):
                for h, m in enumerate("fs"):
                    big = a[f"L0_gnn_W{m}{l + 1}"]
                    w(k.wc[0:C, l, h * C:(h + 1) * C], big[0:C, :])
                    w(k.wc[0:C, l, (2 + h) * C:(3 + h) * C], big[C:2 * C, :])
                    w(k.wc[C:C + 1, l, h * C:(h + 1) * C], a[f"L0_gnn_b{m}{l + 1}"].rearrange("(p c) -> p c", p=1))
            for j, v in enumerate(("b0", "g0", "beta0", "b1", "gf", "betaf")):
                act.dma_start(k.gvec[:, j, :], a["L1_gnn_" + v].rearrange("(p c) -> p c", p=1).broadcast_to([P, C])).then_inc(s_w, 16)
            for c in range(CH):
                if c >= 2:
                    act.wait_ge(s_red, NRED * (c - 1))
                t0 = c * P
                if c < CH - 1:
                    act.dma_start(ea[c % 2], a["edge_attr_16"][t0 * P:(t0 + P) * P, :].rearrange("(p e) d -> p e d", e=P)).then_inc(s_ea[c % 2], 16)
                else:
                    act.wait_ge(s_red, NRED * c + 1)
                    act.dma_start(ea[c % 2][0:part], a["edge_attr_16"][t0 * P:FULL * P, :].rearrange("(p e) d -> p e d", e=P)).then_inc(s_ea[c % 2], 16)
                    act.dma_start(ea[c % 2][part:part + 1, 0:tail, :], a["edge_attr_16"][FULL * P:E, :].rearrange("(p e) d -> p e d", p=1)).then_inc(s_ea[c % 2], 16)
            act.wait_ge(s_w, 16 * (10 + 12 + 6))
            for b in range(NBATCH):
                act.wait_ge(s_tr, b + 1)
                bank = k.psum[b % 2]
                nc.scalar.activation(k.dst_rel[:, b * P:(b + 1) * P], bank[:, 0:P], ACT.Copy).then_inc(s_out, 1)
                for l in range(2):
                    nc.scalar.activation(k.ae[:, b * P:(b + 1) * P, l], bank[:, (2 + l) * P:(3 + l) * P], ACT.Copy).then_inc(s_out, 1)

        @block.vector
        def _(v):
            link = Chain(v, s_ch)
            nc.vector.memset(k.wc[C:C + 1, :, :], 0.0).then_inc(s_pad, 1)
            nc.vector.memset(k.xt[C:C + 1, :, :], 1.0).then_inc(s_pad, 1)
            v.wait_ge(s_const, NCONST)
            v.wait_ge(s_w, 16 * (10 + 12 + 6))
            for l in range(2):
                link(nc.vector.tensor_copy(aeb[:, l, :], att[:, 3 * l + 2:3 * l + 3].broadcast_to([C, P])))
            v.wait_ge(s_wt, 1)
            nc.vector.tensor_copy(wet.rearrange("p l d -> p (l d)"), k.psum[7][0:C, 0:2 * D]).then_inc(s_wtc, 1)
            nc.vector.tensor_copy(wt.rearrange("p l c -> p (l c)"), k.psum[7][0:C, P:P + 2 * C]).then_inc(s_wtc, 1)
            v.wait_ge(s_wv, 1)
            link(nc.vector.tensor_copy(vb.rearrange("p l d -> p (l d)"), k.psum[6][:, 0:2 * D]))
            for l in range(2):
                link(nc.vector.tensor_copy(k.gw[:, l, C:C + 2], k.psum[6][0:C, P + 2 * l:P + 2 * l + 2]))
            v.wait_ge(s_int, 16 * (6 + 2 * CH + 1))
            link(nc.vector.tensor_scalar(blk, dint[:, :, P - 1], 7, None, ALU.arith_shift_right))
            link(nc.vector.tensor_copy(thr, blk))
            nc.vector.tensor_tensor(thr, thr, tile1, ALU.add).then_inc(s_thr, 1)
            v.wait_ge(s_thr, 1)
            for c in range(CH):
                if c >= 2:
                    v.wait_ge(s_cnt, c - 1)
                nc.vector.tensor_scalar(cmp[c % 2], iota_s, thr[:, c:c + 1], None, ALU.is_ge).then_inc(s_cmp, 1)
            nc.vector.tensor_copy(rows[:, :, KEY:KEY + P], dint)
            nc.vector.tensor_copy(rows[:, :, SRC:SRC + P], sint)
            nc.vector.tensor_copy(rows[:, :, PREV:PREV + 1], neigh[:, :, 0:1])
            nc.vector.tensor_copy(rows[:, :, NEXT:NEXT + 1], neigh[:, :, 1:2]).then_inc(s_rows, 1)
            v.wait_ge(s_cnt, CH)
            for j in range(4):
                link(nc.vector.tensor_copy(t_row[:, j * STEPS // 4:(j + 1) * STEPS // 4], k.psum[2 + j][0:1, 0:STEPS // 4]))
            nc.vector.tensor_tensor(b_row, iota_s[0:1, :], t_row, ALU.subtract).then_inc(s_trow, 1)
            v.wait_ge(s_trow, 1)
            for row, width in ((ACC_ROW, AW), (TAB_ROW, 2 * C), (SPREAD_ROW, 2)):
                link(nc.vector.tensor_scalar(k.offsets[row:row + 1, :], b_row, float(NB - 1), float(width), ALU.min, ALU.mult))
            v.wait_ge(s_tcol, 1)
            link(nc.vector.tensor_copy(tcol, k.psum[6][:, 256:256 + CH]))
            nc.vector.tensor_copy(tidx, tcol).then_inc(s_tidx, 1)
            link(nc.vector.tensor_tensor(off, step_col, tcol, ALU.subtract))
            link(nc.vector.tensor_scalar(off, off, float(P), None, ALU.mult))
            for c in range(CH):
                if c == CH - 1:
                    v.wait_ge(s_red, NRED * c)
                    nc.vector.memset(ea[c % 2], 0.0).then_inc(s_red, 1)
                    v.wait_ge(s_ea[c % 2], 16 * (c // 2) + 32)
                else:
                    v.wait_ge(s_ea[c % 2], 16 * (c // 2 + 1))
                for l in range(2):
                    done = 2 * c + l
                    wait(v, s_red, done + (c == CH - 1))
                    nc.vector.tensor_tensor(prod, ea[c % 2], vb[:, l, :].unsqueeze(1).broadcast_to([P, P, D]), ALU.mult).then_inc(s_prod, 1)
                    v.wait_ge(s_prod, done + 1)
                    nc.vector.tensor_reduce(rows[:, c, AE + l * P:AE + (l + 1) * P], prod, AX.X, ALU.add).then_inc(s_red, 1)
            for b in range(NBATCH):
                v.wait_ge(s_g[b % 2], 16 * (b // 2 + 1))
                nc.vector.tensor_copy(k.keys[:, b * (P + 2):(b + 1) * (P + 2)], gath[b % 2][:, 0:P + 2]).then_inc(s_rel, 1)
                wait(v, s_tr, b - 1)
                nc.vector.tensor_scalar(rel[b % 2], gath[b % 2][:, KEY:KEY + P], off[:, b:b + 1], None, ALU.subtract).then_inc(s_rel, 1)
                v.wait_ge(s_tr, b + 1)
                v.wait_ge(s_out, 4 * b + 3)
                nc.vector.tensor_copy(k.src_idx[:, b * P:(b + 1) * P], k.psum[b % 2][:, P:2 * P]).then_inc(s_out, 1)

        @block.tensor
        def _(pe):
            pe.wait_ge(s_const, NCONST)
            pe.wait_ge(s_w, 16 * (10 + 12 + 6))
            for l in range(2):
                nc.tensor.transpose(k.psum[7][0:C, l * D:(l + 1) * D], we[:, l, :], k.ident[0:D, 0:D])
            for l in range(2):
                last = nc.tensor.transpose(k.psum[7][0:C, P + l * C:P + (l + 1) * C], k.gw[:, l, 0:C], k.ident[0:C, 0:C])
            last.then_inc(s_wt, 1)
            pe.wait_ge(s_wtc, 2)
            pe.wait_ge(s_ch, 2)
            for l in range(2):
                nc.tensor.matmul(k.psum[6][:, l * D:(l + 1) * D], aeb[:, l, :], wet[:, l, :], start=True, stop=True)
            for l in range(2):
                last = nc.tensor.matmul(k.psum[6][0:C, P + 2 * l:P + 2 * l + 2], wt[:, l, :], att[:, 3 * l:3 * l + 2], start=True, stop=True)
            last.then_inc(s_wv, 1)
            for c in range(CH):
                pe.wait_ge(s_cmp, c + 1)
                for j in range(4):
                    w = STEPS // 4
                    last = nc.tensor.matmul(k.psum[2 + j][0:1, 0:w], ones_bf, cmp[c % 2][:, j * w:(j + 1) * w], start=c == 0, stop=c == CH - 1)
                last.then_inc(s_cnt, 1)
            pe.wait_ge(s_trow, 1)
            pe.wait_ge(s_ch, 5)
            for b in range(NBATCH):
                last = nc.tensor.transpose(k.psum[6][:, 256 + b:257 + b], t_row[:, b * P:(b + 1) * P], k.ident[0:1, 0:1])
            last.then_inc(s_tcol, 1)
            for b in range(NBATCH):
                pe.wait_ge(s_g[b % 2], 16 * (b // 2 + 1))
                pe.wait_ge(s_rel, 2 * b + 2)
                wait(pe, s_out, 4 * (b - 1))
                g = gath[b % 2]
                for j, m in enumerate((rel[b % 2], g[:, SRC:SRC + P], g[:, AE:AE + P], g[:, AE + P:AE + 2 * P])):
                    last = nc.tensor.transpose(k.psum[b % 2][:, j * P:(j + 1) * P], m, k.ident[:, :])
                last.then_inc(s_tr, 1)


def cg_tables(k, layer):
    nc = k.nc
    k.next_stage()
    n = f"cgt{layer}_"
    s_z, s_h, s_t, s_tc, s_m, s_p, s_q, s_st = (k.sem(n + x) for x in ("zero", "h", "t", "tc", "m", "p", "q", "store"))
    p_tab = k.big[:, 0:NB * 2 * C]
    q_stage = k.wide[:, 0:NB * 2 * C]
    q_rows = k.q_table.rearrange("(b p) c -> p b c", p=P)

    h_stage = k.work[:, 0:2 * P].rearrange("p (j c) -> p j c", c=P)

    with nc.Block() as block:
        @block.gpsimd
        def _(pool):
            def body(b, j):
                wait(pool, s_t, b - 1)
                nc.gpsimd.tensor_copy(h_stage[:, j, 0:C], flat(k.node_a[:, ds(b, 1), :])).then_inc(s_h, 1)
            nc.gpsimd.memset(k.work[:, 0:2 * P], 0.0).then_inc(s_z, 1)
            pool.wait_ge(s_z, 1)
            body(0, 0)
            body(1, 1)
            with pool.Fori(1, NB // 2) as i:
                body(i * 2, 0)
                body(i * 2 + 1, 1)

        @block.tensor
        def _(pe):
            def body(b, j):
                pe.wait_ge(s_h, b + 1)
                wait(pe, s_tc, b - 1)
                nc.tensor.transpose(k.psum[j][:, 0:P], h_stage[:, j, :], k.ident[:, :]).then_inc(s_t, 1)
                pe.wait_ge(s_tc, b + 1)
                wait(pe, s_p, b - 1)
                wait(pe, s_q, b - 1)
                nc.tensor.matmul(k.psum[2 + j][:, 0:4 * C], k.xt[:, j, :], k.wc[:, layer, :], start=True, stop=True).then_inc(s_m, 1)
            body(0, 0)
            body(1, 1)
            with pe.Fori(1, NB // 2) as i:
                body(i * 2, 0)
                body(i * 2 + 1, 1)

        @block.scalar
        def _(act):
            def body(b, j):
                act.wait_ge(s_t, b + 1)
                wait(act, s_m, b - 1)
                nc.scalar.activation(k.xt[0:C, j, :], k.psum[j][0:C, 0:P], ACT.Copy).then_inc(s_tc, 1)
                act.wait_ge(s_m, b + 1)
                nc.scalar.activation(p_tab[:, ds(b * 2 * C, 2 * C)], k.psum[2 + j][:, 0:2 * C], ACT.Copy).then_inc(s_p, 1)
            body(0, 0)
            body(1, 1)
            with act.Fori(1, NB // 2) as i:
                body(i * 2, 0)
                body(i * 2 + 1, 1)

        @block.vector
        def _(v):
            def body(b, j):
                v.wait_ge(s_p, b + 1)
                nc.vector.tensor_copy(q_stage[:, ds(b * 2 * C, 2 * C)], k.psum[2 + j][:, 2 * C:4 * C]).then_inc(s_q, 1)
            with v.Fori(0, NB // 2) as i:
                body(i * 2, 0)
                body(i * 2 + 1, 1)

        @block.sync
        def _(sp):
            k.clear_old(sp)
            with sp.Fori(0, NB // 14) as i:
                sp.wait_ge(s_q, i * 14 + 14)
                sp.dma_start(q_rows[:, ds(i * 14, 14), :],
                             q_stage[:, ds(i * 14 * 2 * C, 14 * 2 * C)].rearrange("p (b c) -> p b c", c=2 * C)).then_inc(s_st, 16)
            sp.wait_ge(s_st, 16 * (NB // 14))


def build_onehot(nc, k, to, s):
    return nc.vector.tensor_tensor(to, k.iota[:, :].unsqueeze(1).broadcast_to([P, GROUP, P]),
                                   k.dst_rel[:, ds(s, GROUP)].unsqueeze(2).broadcast_to([P, GROUP, P]), ALU.is_equal)


def load_offsets(k, eng, row, first, count, step):
    _, values = k.nc.values_load_multi_w_load_instructions(
        k.offsets[row:row + 1, ds(first, count)], engines=[eng.engine], min_val=0, max_val=(NB - 1) * step,
        skip_runtime_bounds_check_because="setup takes the minimum with the last block's offset")
    return values


def counts(eng, first, lo, hi):
    return {c: first + c if isinstance(first, int) else eng.snap(first + c) for c in range(lo, hi + 1)}


def pipelined(eng, iterations, emit):
    emit(0, True, False)
    with eng.Fori(1, iterations) as it:
        emit(it, False, False)
    emit(iterations, False, True)


def stages(u, first, last, *lagged):
    for lag, stage in lagged:
        c = u - lag
        if not (first and c < 0) and not (last and c >= 0):
            stage(c)


def cg_edges(k, layer):
    nc = k.nc
    k.next_stage()
    n = f"cge{layer}_"
    (s_zero, s_S, s_T, s_Tc, s_X, s_ln, s_softf, s_softs, s_sig, s_msg, s_agg, s_add, s_acc, s_idx, s_act) = (
        k.sem(n + x) for x in ("zero", "onehot", "trans", "trans_sb", "pre", "ln", "soft_f", "soft_s", "sig", "msg", "agg", "add", "acc", "idx", "act"))
    s_row, row_base = k.rows, list(k.row_base)
    k.row_base = [r + GROUPS // UNROLL * GROUP * 16 for r in row_base]
    s_turn = k.sem(n + "turn")
    p_tab = k.big[:, 0:NB * 2 * C]
    ring = k.big[:, NB * 2 * C:NB * 2 * C + RING].rearrange("p (u i c) -> p u i c", u=UNROLL, c=2 * C)
    acc = k.wide[:, NB * C:NB * (C + AW)]
    soft = k.work[:, 0:8 * P].rearrange("p (u i c) -> p u i c", u=2, c=2 * C)
    pre = [k.psum[2 + j][:, :].rearrange("p (i c) -> p i c", c=2 * C) for j in range(2)]
    width = AW if layer == 0 else C
    ITERS = GROUPS // UNROLL
    f_half, s_half = slice(0, C), slice(C, 2 * C)

    with nc.Block() as block:
        @block.sync
        def _(sp):
            k.clear_old(sp)

        @block.gpsimd
        def _(pool):
            def batch(b):
                for s in range(P):
                    u = s // GROUP % UNROLL
                    if s % GROUP == 0:
                        wait(pool, s_X, b * BGROUPS + (s // GROUP - UNROLL + 1))
                        pool.sem_inc(s_turn, 1)
                    if s % HALF == HALF // 2:
                        start = b * P + (HALF if s < HALF else P)
                        other = (HALF if s < HALF else 0)
                        nc.gpsimd.tensor_copy(k.idx_stage[:, other:other + HALF], k.src_idx[:, ds(start, HALF)]).then_inc(s_idx, 1)
                    if s % HALF == 0:
                        pool.wait_ge(s_idx, b * 2 + (s // HALF + 1))
                        pool.sem_inc(s_turn, 1)
                    pool.indirect_dma_start(out=ring[:, u, s % GROUP, :], out_offset=None, in_=k.q_table,
                                            in_offset=bass.IndirectOffsetOnAxis(ap=k.idx_stage[:, s:s + 1], axis=0)).then_inc(s_row[u], 16)
            nc.gpsimd.tensor_copy(k.idx_stage[:, 0:HALF], k.src_idx[:, 0:HALF]).then_inc(s_idx, 1)
            batch(0)
            with pool.Fori(1, NBATCH) as b:
                batch(b)

        @block.vector
        def _(v):
            nc.vector.memset(k.acc, 0.0).then_inc(s_acc, 1)
            if layer == 0:
                nc.vector.memset(k.msg[:, :, :, C + 2:C + 3], 1.0).then_inc(s_zero, 1)

            def iteration(it, first, last):
                n = counts(v, it * UNROLL, -4, 3)

                def onehot(c):
                    wait(v, s_agg, n[c - 3])
                    build_onehot(nc, k, k.onehot[:, c % UNROLL], it * ITER + c * GROUP).then_inc(s_S, 1)

                def softs(c):
                    j = c % 2
                    wait(v, s_ln, n[c + 1])
                    nc.vector.scalar_tensor_tensor(soft[:, j, :, f_half], pre[j][:, :, f_half], 0.0, soft[:, j, :, f_half], ALU.min, ALU.subtract).then_inc(s_softf, 1)
                    nc.vector.scalar_tensor_tensor(soft[:, j, :, s_half], pre[j][:, :, s_half], 0.0, soft[:, j, :, s_half], ALU.max, ALU.add).then_inc(s_softs, 1)

                def message(c):
                    j = c % 2
                    wait(v, s_sig, n[c + 1])
                    wait(v, s_softs, n[c + 1])
                    nc.vector.tensor_tensor(k.msg[:, c % UNROLL, :, 0:C], soft[:, j, :, f_half], soft[:, j, :, s_half], ALU.mult).then_inc(s_msg, 1)

                def accumulate(c):
                    at = load_offsets(k, v, ACC_ROW, it * ITER + c * GROUP, GROUP, AW)
                    wait(v, s_agg, n[c + 1])
                    wait(v, s_acc, n[c + 1])
                    for i in range(GROUP):
                        if i:
                            v.wait_ge(s_add, i)
                        to = acc[:, ds(at[i], width)]
                        nc.vector.tensor_tensor(to, to, k.psum[4 + c % 2][:, i * P:i * P + width], ALU.add).then_inc(s_add if i < GROUP - 1 else s_acc, 1)
                    v.sem_clear(s_add)

                for u in range(UNROLL):
                    stages(u, first, last, (0, onehot), (2, softs), (3, message), (4, accumulate))
            pipelined(v, ITERS, iteration)

        @block.scalar
        def _(act):
            act.preload_act_table_set("natural_log_exp_and_others")

            def iteration(it, first, last):
                n = counts(act, it * UNROLL, -4, 4)

                def copy_t(c):
                    wait(act, s_T, n[c + 1])
                    wait(act, s_X, n[c - 1])
                    nc.scalar.activation(k.onehot_t[:, c % 2, :, :], k.psum[c % 2][:, :].rearrange("p (i c) -> p i c", c=P), ACT.Copy).then_inc(s_Tc, 1)

                def logs(c):
                    j = c % 2
                    wait(act, s_X, n[c + 1])
                    wait(act, s_msg, n[c - 1])
                    nc.scalar.activation(soft[:, j], pre[j], ACT.Abs).then_inc(s_act, 1)
                    act.wait_ge(s_act, 1)
                    nc.scalar.activation(soft[:, j], soft[:, j], ACT.Exp, scale=-1.0).then_inc(s_act, 1)
                    act.wait_ge(s_act, 2)
                    act.sem_clear(s_act)
                    nc.scalar.activation(soft[:, j], soft[:, j], ACT.Ln, bias=1.0).then_inc(s_ln, 1)

                def sigmoids(c):
                    wait(act, s_softf, n[c + 1])
                    if layer == 0:
                        nc.scalar.activation(k.msg[:, c % UNROLL, :, C:C + 2], k.ae[:, ds(it * ITER + c * GROUP, GROUP), :], ACT.Copy)
                    nc.scalar.activation(soft[:, c % 2, :, f_half], soft[:, c % 2, :, f_half], ACT.Exp).then_inc(s_sig, 1)

                for u in range(UNROLL):
                    stages(u, first, last, (0, copy_t), (2, sigmoids), (1, logs))
            pipelined(act, ITERS, iteration)

        @block.tensor
        def _(pe):
            def iteration(it, first, last):
                n = counts(pe, it * UNROLL, -4, 4)
                gathered = it * (16 * GROUP)

                def transposes(c):
                    wait(pe, s_S, n[c + 1])
                    wait(pe, s_Tc, n[c - 1])
                    for i in range(GROUP):
                        last_one = nc.tensor.transpose(k.psum[c % 2][:, i * P:(i + 1) * P], k.onehot[:, c % UNROLL, i, :], k.ident[:, :])
                    last_one.then_inc(s_T, 1)

                def form(c):
                    j, slot = c % 2, c % UNROLL
                    at = load_offsets(k, pe, TAB_ROW, it * ITER + c * GROUP, GROUP, 2 * C)
                    pe.wait_ge(s_row[slot], gathered + (16 * GROUP * (1 if c >= 0 else 0) + row_base[slot]))
                    wait(pe, s_softs, n[c - 1])
                    nc.tensor.matmul(k.psum[2 + j][:, :], k.ident[:, :], ring[:, slot].rearrange("p i c -> p (i c)"), start=True, stop=False)
                    wait(pe, s_Tc, n[c + 1])
                    for i in range(GROUP):
                        last_one = nc.tensor.matmul(k.psum[2 + j][:, i * P:(i + 1) * P], k.onehot_t[:, j, i, :],
                                                    p_tab[:, ds(at[i], 2 * C)], start=False, stop=i == GROUP - 1)
                    last_one.then_inc(s_X, 1)

                def segment_sum(c):
                    wait(pe, s_msg, n[c + 1])
                    wait(pe, s_acc, n[c])
                    for i in range(GROUP):
                        last_one = nc.tensor.matmul(k.psum[4 + c % 2][:, i * P:i * P + width], k.onehot[:, c % UNROLL, i, :],
                                                    k.msg[:, c % UNROLL, i, 0:width], start=True, stop=True)
                    last_one.then_inc(s_agg, 1)

                for u in range(UNROLL):
                    stages(u, first, last, (0, transposes), (1, form), (3, segment_sum))
            if layer == 0:
                pe.wait_ge(s_zero, 1)
            pipelined(pe, ITERS, iteration)


def layer_norm(nc, k, v, link, sq, s_act_in, s_act_out, n):
    mean, var = k.node_col[:, 0, :], k.node_col[:, 1, :]
    link(nc.vector.tensor_reduce(mean, k.node_a, AX.X, ALU.add))
    link(nc.vector.tensor_scalar(mean, mean, 1.0 / C, None, ALU.mult))
    nc.vector.tensor_tensor(k.node_a, k.node_a, mean.unsqueeze(2).broadcast_to([P, NB, C]), ALU.subtract).then_inc(s_act_in, 1)
    v.wait_ge(s_act_out, n + 1)
    link(nc.vector.tensor_reduce(var, sq, AX.X, ALU.add))
    nc.vector.tensor_scalar(var, var, 1.0 / C, EPS, ALU.mult, ALU.add).then_inc(s_act_in, 1)
    v.wait_ge(s_act_out, n + 2)
    link(nc.vector.reciprocal(var, var))
    link(nc.vector.tensor_tensor(k.node_a, k.node_a, var.unsqueeze(2).broadcast_to([P, NB, C]), ALU.mult))


def layer_norm_act(nc, k, act, sq, s_act_in, s_act_out, n):
    act.wait_ge(s_act_in, n + 1)
    nc.scalar.activation(sq, k.node_a, ACT.Square).then_inc(s_act_out, 1)
    act.wait_ge(s_act_in, n + 2)
    nc.scalar.activation(k.node_col[:, 1, :], k.node_col[:, 1, :], ACT.Sqrt).then_inc(s_act_out, 1)


def cg_finish(k, layer, x):
    nc = k.nc
    k.next_stage()
    n = f"cgf{layer}_"
    s_x, s_ch, s_in, s_out, s_st = (k.sem(n + c) for c in ("x", "chain", "act_in", "act_out", "store"))
    sq = k.big[:, 0:NB * C].rearrange("p (b c) -> p b c", c=C)
    with nc.Block() as block:
        @block.vector
        def _(v):
            link = Chain(v, s_ch)
            if layer == 0:
                nc.vector.tensor_copy(k.loop_sum[:, :, :], k.acc[:, :, C:AW])
            link(nc.vector.tensor_tensor(k.node_a, k.node_a, k.acc[:, :, 0:C], ALU.add))
            if layer == 0:
                link(nc.vector.tensor_scalar(k.node_a, k.node_a, 0.0, None, ALU.max))
                return
            nc.vector.memset(k.node_b[:, NB - 1, :], 0.0).then_inc(s_in, 1)
            v.wait_ge(s_x, 32)
            link(nc.vector.tensor_scalar(k.node_a, k.node_a, 0.0, None, ALU.max))
            link(nc.vector.tensor_tensor(k.node_a, k.node_a, k.node_b, ALU.add))
            layer_norm(nc, k, v, link, sq, s_in, s_out, 0)

        if layer == 1:
            @block.scalar
            def _(act):
                layer_norm_act(nc, k, act, sq, s_in, s_out, 1)

            @block.sync
            def _(sp):
                sp.wait_ge(s_in, 1)
                load_nodes(sp, k.node_b, x, s_x)
                sp.wait_ge(s_ch, CG_LN_LINKS)
                sp.dma_start(k.x1_dram.rearrange("(b p) c -> p b c", p=P), k.node_a).then_inc(s_st, 16)
                sp.wait_ge(s_st, 16)


CG_LN_LINKS = 8


def gat_tables(k, layer):
    nc = k.nc
    k.next_stage()
    n = f"gat{layer}_t_"
    s_z, s_h, s_t, s_tc, s_m, s_p, s_q, s_st, s_ch = (k.sem(n + x) for x in ("zero", "h", "t", "tc", "m", "p", "q", "store", "chain"))
    stage = k.big[:, 0:NB * TW].rearrange("p (b c) -> p b c", c=TW)
    rows = k.xl_table.rearrange("(b p) c -> p b c", p=P)
    a_src, a_dst, tmp, mean = (k.node_col[:, i, :] for i in range(4))

    h_stage = k.work[:, 0:2 * P].rearrange("p (j c) -> p j c", c=P)

    with nc.Block() as block:
        @block.gpsimd
        def _(pool):
            def body(b, j):
                wait(pool, s_t, b - 1)
                nc.gpsimd.tensor_copy(h_stage[:, j, 0:C], flat(k.node_a[:, ds(b, 1), :])).then_inc(s_h, 1)
            nc.gpsimd.memset(k.work[:, 0:2 * P], 0.0).then_inc(s_z, 1)
            pool.wait_ge(s_z, 1)
            body(0, 0)
            body(1, 1)
            with pool.Fori(1, NB // 2) as i:
                body(i * 2, 0)
                body(i * 2 + 1, 1)

        @block.tensor
        def _(pe):
            def body(b, j):
                pe.wait_ge(s_h, b + 1)
                wait(pe, s_tc, b - 1)
                nc.tensor.transpose(k.psum[j][:, 0:P], h_stage[:, j, :], k.ident[:, :]).then_inc(s_t, 1)
                pe.wait_ge(s_tc, b + 1)
                wait(pe, s_p, b - 1)
                wait(pe, s_q, b - 1)
                nc.tensor.matmul(k.psum[2 + j][:, 0:C + 2], k.xt[0:C, j, :], k.gw[:, layer, :], start=True, stop=True).then_inc(s_m, 1)
            body(0, 0)
            body(1, 1)
            with pe.Fori(1, NB // 2) as i:
                body(i * 2, 0)
                body(i * 2 + 1, 1)

        @block.scalar
        def _(act):
            def body(b, j):
                act.wait_ge(s_t, b + 1)
                wait(act, s_m, b - 1)
                nc.scalar.activation(k.xt[0:C, j, :], k.psum[j][0:C, 0:P], ACT.Copy).then_inc(s_tc, 1)
                act.wait_ge(s_m, b + 1)
                nc.scalar.activation(flat(stage[:, ds(b, 1), :]), k.psum[2 + j][:, 0:TW], ACT.Copy).then_inc(s_p, 1)
            body(0, 0)
            body(1, 1)
            with act.Fori(1, NB // 2) as i:
                body(i * 2, 0)
                body(i * 2 + 1, 1)

        @block.vector
        def _(v):
            def body(b, j):
                v.wait_ge(s_p, b + 1)
                nc.vector.tensor_copy(flat(k.node_b[:, ds(b, 1), :]), k.psum[2 + j][:, 0:C])
                nc.vector.tensor_copy(k.spread[:, ds(b, 1), 0:1], k.psum[2 + j][:, C + 1:C + 2].unsqueeze(2)).then_inc(s_q, 1)
            with v.Fori(0, NB // 2) as i:
                body(i * 2, 0)
                body(i * 2 + 1, 1)
            link = Chain(v, s_ch)
            v.wait_ge(s_q, NB)
            link(nc.vector.tensor_tensor(a_src, stage[:, :, C], k.spread[:, :, 0], ALU.add))
            link(nc.vector.tensor_scalar(tmp, k.loop_sum[:, :, 2], 1.0, None, ALU.max))
            link(nc.vector.reciprocal(tmp, tmp))
            link(nc.vector.tensor_tensor(mean, k.loop_sum[:, :, layer], tmp, ALU.mult))
            link(nc.vector.tensor_tensor(a_src, a_src, mean, ALU.add))
            link(nc.vector.scalar_tensor_tensor(k.spread[:, :, 1], a_src, SLOPE, a_src, ALU.mult, ALU.max))

        @block.sync
        def _(sp):
            k.clear_old(sp)
            with sp.Fori(0, NB // 14) as i:
                sp.wait_ge(s_p, i * 14 + 14)
                sp.dma_start(rows[:, ds(i * 14, 14), :], stage[:, ds(i * 14, 14), :]).then_inc(s_st, 16)
            sp.wait_ge(s_st, 16 * (NB // 14))


def gat_edges(k, layer):
    nc = k.nc
    k.next_stage()
    n = f"gat{layer}_e_"
    (s_zero, a_S, a_T, a_Tc, a_X, s_sc, s_x3, s_x3c, s_cc, s_cr, s_tu, s_tub, s_dif, s_exp, s_w, s_wt, s_wsw,
     s_fb, s_fv, s_fe, s_done, e_S, e_m, e_agg, e_add, e_acc, s_ch, s_idx) = (
        k.sem(n + x) for x in (
            "zero", "a_onehot", "a_trans", "a_trans_sb", "a_spread", "scores", "scores_t", "scores_t_sb", "cols", "rows",
            "carry", "carry_t", "diff", "exp", "weights", "weights_t", "weights_sb", "factor_ps", "factor_log", "factor",
            "rescaled", "e_onehot", "e_msg", "e_agg", "e_add", "e_acc", "chain", "idx"))
    s_gat, gat_base = [k.rows[0:2], k.rows[2:4]], [k.row_base[0:2], k.row_base[2:4]]
    turns = [(NBATCH + 1) // 2, NBATCH // 2]
    k.row_base = [r + turns[i // 2] * HALF * 16 for i, r in enumerate(k.row_base)]
    s_turn = k.sem(n + "turn")
    spread_sems = [[k.sem(f"{n}first{x}") for x in range(4)], [a_S, a_T, a_Tc, a_X]]
    acc = k.wide[:, NB * C:NB * (C + AW)]
    buf = [k.big[:, i * P * TW:(i + 1) * P * TW].rearrange("p (s c) -> p s c", c=TW) for i in range(2)]
    w = k.work
    x3 = w[:, 0:3 * P].rearrange("p (j s) -> p j s", s=P)
    x3t = w[:, 3 * P:6 * P].rearrange("p (j e) -> p j e", e=P)
    valid, vneg = w[:, 6 * P:7 * P], w[:, 7 * P:8 * P]
    neq = w[:, 8 * P:9 * P + 1]
    pen = w[:, 9 * P + 8:10 * P + 9]
    fwd = w[:, 11 * P:12 * P]
    seg = w[:, 12 * P:13 * P]
    far = w[:, 13 * P:14 * P]
    wx = w[:, 14 * P:16 * P].rearrange("p (j e) -> p j e", e=P)
    wsw = w[:, 16 * P:18 * P].rearrange("p (s j) -> p s j", j=2)
    cols = w[:, 18 * P:18 * P + 4]
    carry = w[:, 18 * P + 4:18 * P + 6]
    fac = w[:, 18 * P + 6:18 * P + 7]
    single = w[:, 18 * P + 7:18 * P + 8]
    fpair = w[0:1, 18 * P + 8:18 * P + 10]
    at = 2 * P * TW
    t_row = k.big[0:1, at:at + P + 1]
    u_row = k.big[0:1, at + 136:at + 136 + P + 1]
    crow = k.big[0:1, at + 272:at + 272 + 4 * P]
    a_onehot = k.big[:, at + 272 + 4 * P:at + 272 + 4 * P + ITER * P].rearrange("p (u i c) -> p u i c", u=UNROLL, c=P)
    bank_ad = k.psum[2][:, 0:2 * P].rearrange("p (s j) -> p s j", j=2)
    LINKS = 26
    BIT = BGROUPS // UNROLL
    OUTER = (NBATCH - 1) // 2

    def over_batches(eng, batch):
        batch(0, 0, 0)
        with eng.Fori(0, OUTER - 1) as j:
            batch(j * 2 + 1, 1, j)
            batch(j * 2 + 2, 0, j + 1)
        batch(NBATCH - 2, 1, OUTER - 1)
        batch(NBATCH - 1, 0, OUTER)

    def ends(b):
        return isinstance(b, int) and b == NBATCH - 1

    with nc.Block() as block:
        @block.sync
        def _(sp):
            k.clear_old(sp)

        @block.gpsimd
        def _(pool):
            def batch(b, p, turn):
                wait(pool, e_m, (b - 1) * BGROUPS)
                for s in range(P):
                    half = s // HALF
                    if s == HALF // 2:
                        if p == 1 or not isinstance(b, int) or b:
                            pool.wait_ge(s_gat[1 - p][1], turn * (16 * HALF) + (p * 16 * HALF + gat_base[1 - p][1]))
                            pool.sem_inc(s_turn, 1)
                        nc.gpsimd.tensor_copy(k.idx_stage[:, HALF:P], k.src_idx[:, ds(b * P + HALF, HALF)]).then_inc(s_idx, 1)
                    if s == HALF + HALF // 2:
                        pool.wait_ge(s_gat[p][0], turn * (16 * HALF) + (16 * HALF + gat_base[p][0]))
                        pool.sem_inc(s_turn, 1)
                        nc.gpsimd.tensor_copy(k.idx_stage[:, 0:HALF], k.src_idx[:, ds(b * P + P, HALF)]).then_inc(s_idx, 1)
                    if s % HALF == 0:
                        pool.wait_ge(s_idx, b * 2 + half + 1)
                        pool.sem_inc(s_turn, 1)
                    pool.indirect_dma_start(out=buf[p][:, s, :], out_offset=None, in_=k.xl_table,
                                            in_offset=bass.IndirectOffsetOnAxis(ap=k.idx_stage[:, s:s + 1], axis=0)).then_inc(s_gat[p][half], 16)
            nc.gpsimd.tensor_copy(k.idx_stage[:, 0:HALF], k.src_idx[:, 0:HALF]).then_inc(s_idx, 1)
            batch(0, 0, 0)
            batch(1, 1, 0)
            with pool.Fori(1, OUTER) as j:
                batch(j * 2, 0, j)
                batch(j * 2 + 1, 1, j)
            batch(NBATCH - 1, 0, OUTER)

        @block.vector
        def _(v):
            nc.vector.memset(k.acc, 0.0).then_inc(e_acc, 1)
            nc.vector.memset(t_row[:, P:P + 1], BIG_NEG).then_inc(s_zero, 1)
            nc.vector.memset(u_row[:, P:P + 1], BIG_NEG).then_inc(s_zero, 1)
            v.wait_ge(s_zero, 2)

            def spread(sems, n, step, c):
                made, turned = sems[0:2]
                wait(v, turned, n[c - 3])
                build_onehot(nc, k, a_onehot[:, c], step + c * GROUP).then_inc(made, 1)

            def spread_first(it, first, last):
                n = counts(v, it * UNROLL, -3, 0)
                for u in range(UNROLL):
                    stages(u, first, last, (0, lambda c: spread(spread_sems[0], n, it * ITER, c)))
            pipelined(v, BIT, spread_first)

            def batch(b, p, turn):
                first_group = b * BGROUPS
                gather = buf[p]
                link = Chain(v, s_ch, b * LINKS)
                key = k.keys[:, ds(b * (P + 2), P + 2)]
                rel = k.dst_rel[:, ds(b * P, P)]
                link(nc.vector.tensor_scalar(valid, rel, 0.0, None, ALU.is_ge))
                link(nc.vector.scalar_tensor_tensor(valid, rel, float(P), valid, ALU.is_lt, ALU.mult))
                link(nc.vector.tensor_scalar(vneg, valid, 1.0, -BIG_NEG, ALU.subtract, ALU.mult))
                link(nc.vector.tensor_tensor(neq, key[:, 1:P + 2], key[:, 0:P + 1], ALU.not_equal))
                link(nc.vector.tensor_scalar(pen, neq, BIG_NEG, None, ALU.mult))
                link(nc.vector.tensor_tensor(single, key[:, 1:2], key[:, P:P + 1], ALU.not_equal))
                link(nc.vector.tensor_scalar(single, single, BIG_NEG, None, ALU.mult))
                link(nc.vector.tensor_tensor(cols[:, 0:1], pen[:, 0:1], single, ALU.add))
                link(nc.vector.tensor_tensor(cols[:, 3:4], pen[:, P:P + 1], single, ALU.add))
                link(nc.vector.tensor_copy(t_row[:, 0:1], t_row[:, P:P + 1]))
                if isinstance(b, int) and b == 0:
                    v.wait_ge(spread_sems[0][3], BGROUPS)
                else:
                    v.wait_ge(a_X, first_group)
                for half in range(2):
                    v.wait_ge(s_gat[p][half], turn * (16 * HALF) + (16 * HALF + gat_base[p][half]))
                link(nc.vector.tensor_tensor(x3[:, 0, :], gather[:, :, C], bank_ad[:, :, 0], ALU.add))
                link(nc.vector.tensor_tensor(x3[:, 0, :], x3[:, 0, :], k.ae[:, ds(b * P, P), layer], ALU.add))
                link(nc.vector.scalar_tensor_tensor(x3[:, 0, :], x3[:, 0, :], SLOPE, x3[:, 0, :], ALU.mult, ALU.max))
                nc.vector.tensor_copy(x3[:, 2, :], bank_ad[:, :, 1])
                link(nc.vector.tensor_tensor(x3[:, 1, :], x3[:, 0, :], bank_ad[:, :, 1], ALU.max))
                link(nc.vector.tensor_tensor(x3, x3, valid.unsqueeze(1).broadcast_to([P, 3, P]), ALU.mult))
                nc.vector.tensor_tensor(x3, x3, vneg.unsqueeze(1).broadcast_to([P, 3, P]), ALU.add).then_inc(s_sc, 1)
                v.wait_ge(s_x3c, b + 1)
                link(nc.vector.tensor_tensor_scan(fwd, pen[:, 0:P], x3t[:, 1, :], BIG_NEG, ALU.add, ALU.max))
                link(nc.vector.tensor_tensor_scan(seg[:, ::-1], pen[:, 1:P + 1][:, ::-1], fwd[:, ::-1], BIG_NEG, ALU.add, ALU.max))
                nc.vector.tensor_copy(cols[:, 1:2], seg[:, P - 1:P]).then_inc(s_cc, 1)
                nc.vector.tensor_copy(cols[:, 2:3], seg[:, 0:1]).then_inc(s_cc, 1)
                v.wait_ge(s_cr, b + 1)
                link(nc.vector.tensor_copy(crow, k.psum[4][0:1, :]))
                nc.vector.tensor_tensor_scan(t_row[:, 1:P + 1], crow[:, 0:P], crow[:, P:2 * P], t_row[:, 0:1], ALU.add, ALU.max).then_inc(s_tu, 1)
                nc.vector.tensor_tensor_scan(u_row[:, 0:P][:, ::-1], crow[:, 3 * P:4 * P][:, ::-1], crow[:, 2 * P:3 * P][:, ::-1],
                                             BIG_NEG, ALU.add, ALU.max).then_inc(s_tu, 1)
                v.wait_ge(s_tub, b + 1)
                link(nc.vector.tensor_tensor(carry[:, 0:1], k.psum[5][:, 0:1], pen[:, 0:1], ALU.add))
                link(nc.vector.tensor_tensor(carry[:, 1:2], k.psum[5][:, 1:2], pen[:, P:P + 1], ALU.add))
                for side, edge in ((0, 1), (1, P)):
                    link(nc.vector.tensor_scalar(far, key[:, 1:P + 1], key[:, edge:edge + 1], BIG_NEG, ALU.not_equal, ALU.mult))
                    link(nc.vector.scalar_tensor_tensor(seg, far, carry[:, side:side + 1], seg, ALU.add, ALU.max))
                nc.vector.tensor_tensor(wx[:, 0, :], x3t[:, 0, :], seg, ALU.subtract).then_inc(s_dif, 1)
                nc.vector.tensor_tensor(wx[:, 1, :], x3t[:, 2, :], seg, ALU.subtract).then_inc(s_dif, 1)
                link(nc.vector.tensor_tensor(fpair[:, 0:1], t_row[:, 0:1], seg[0:1, 0:1], ALU.subtract))
                link(nc.vector.tensor_scalar(neq[0:1, 0:1], neq[0:1, 0:1], -1.0, 1.0, ALU.mult, ALU.add))
                nc.vector.tensor_tensor(fpair[:, 0:1], fpair[:, 0:1], neq[0:1, 0:1], ALU.mult).then_inc(s_fb, 1)
                nc.vector.tensor_copy(fpair[:, 1:2], rel[0:1, 0:1]).then_inc(s_fb, 1)
                v.wait_ge(s_exp, b + 1)
                nc.vector.tensor_tensor(wx[:, 1, :], wx[:, 1, :], neq[:, 1:P + 1], ALU.mult).then_inc(s_w, 1)
                v.wait_ge(s_fv, b + 1)
                nc.vector.tensor_scalar(fac, k.iota_col[:, :], k.psum[5][:, 9:10], k.psum[5][:, 8:9], ALU.is_equal, ALU.mult).then_inc(s_fe, 1)
                start, = load_offsets(k, v, ACC_ROW, b * P, 1, AW)
                v.wait_ge(s_fe, 2 * b + 2)
                v.wait_ge(e_acc, first_group + 1)
                to = acc[:, ds(start, C + 1)]
                nc.vector.tensor_scalar(to, to, fac, None, ALU.mult).then_inc(s_done, 1)

                def sums(it, first, last):
                    n = counts(v, first_group + it * UNROLL, -3, 2)
                    step = (b * BIT + it) * ITER

                    def onehot(c):
                        wait(v, e_agg, n[c - 3])
                        build_onehot(nc, k, k.onehot[:, c], step + c * GROUP).then_inc(e_S, 1)

                    starts = {}

                    def begin(c):
                        starts[c] = load_offsets(k, v, ACC_ROW, step + c * GROUP, GROUP, AW)
                        wait(v, e_agg, n[c + 1])
                        wait(v, e_acc, n[c + 1])
                        add(c, 0)

                    def add(c, i):
                        if i:
                            v.wait_ge(e_add, i)
                        to = acc[:, ds(starts[c][i], C + 2)]
                        nc.vector.tensor_tensor(to, to, k.psum[6 + c % 2][:, i * P:i * P + C + 2], ALU.add).then_inc(e_add if i < GROUP - 1 else e_acc, 1)
                        if i == GROUP - 1:
                            v.sem_clear(e_add)
                    for u in range(UNROLL):
                        stages(u, first, last, (2, begin))
                        if not ends(b):
                            stages(u, first, last, (0, lambda c: spread(spread_sems[1], n, step + P, c)))
                        stages(u, first, last, (2, lambda c: add(c, 1)), (0, onehot), (2, lambda c: add(c, 2)), (2, lambda c: add(c, 3)))
                v.wait_ge(s_done, b + 1)
                pipelined(v, BIT, sums)
                assert link.n == LINKS, link.n
            over_batches(v, batch)

        @block.scalar
        def _(act):
            act.preload_act_table_set("natural_log_exp_and_others")

            def spread(sems, n, c):
                turned, copied, used = sems[1:4]
                wait(act, turned, n[c + 1])
                wait(act, used, n[c - 1])
                nc.scalar.activation(k.onehot_t[:, c % 2, :, :], k.psum[c % 2][:, :].rearrange("p (i c) -> p i c", c=P), ACT.Copy).then_inc(copied, 1)

            def spread_first(it, first, last):
                n = counts(act, it * UNROLL, -1, 4)
                for u in range(UNROLL):
                    stages(u, first, last, (0, lambda c: spread(spread_sems[0], n, c)))
            pipelined(act, BIT, spread_first)

            def batch(b, p, turn):
                first_group = b * BGROUPS
                gather = buf[p]
                act.wait_ge(s_x3, b + 1)
                nc.scalar.activation(x3t, k.psum[3][:, 0:3 * P].rearrange("p (j e) -> p j e", e=P), ACT.Copy).then_inc(s_x3c, 1)
                act.wait_ge(s_dif, 2 * b + 2)
                nc.scalar.activation(wx, wx, ACT.Exp).then_inc(s_exp, 1)
                act.wait_ge(s_fe, 2 * b + 1)
                nc.scalar.activation(fac, fac, ACT.Exp).then_inc(s_fe, 1)
                act.wait_ge(s_wt, b + 1)
                nc.scalar.activation(wsw.rearrange("p s j -> p j s"), k.psum[3][:, 0:2 * P].rearrange("p (j s) -> p j s", s=P), ACT.Copy).then_inc(s_wsw, 1)
                act.wait_ge(s_wsw, b + 1)

                def sums(it, first, last):
                    n = counts(act, first_group + it * UNROLL, -3, 4)

                    def weigh(c):
                        s = it * ITER + c * GROUP
                        wait(act, e_agg, n[c - 3])
                        nc.scalar.activation(k.msg[:, c, :, C:C + 2], wsw[:, ds(s, GROUP), :], ACT.Copy)
                        for i in range(GROUP):
                            last_one = nc.scalar.activation(k.msg[:, c, i, 0:C], flat(gather[:, ds(s + i, 1), 0:C]), ACT.Copy,
                                                            scale=flat(wsw[:, ds(s + i, 1), 0:1]))
                        last_one.then_inc(e_m, 1)
                    for u in range(UNROLL):
                        stages(u, first, last, (0, weigh))
                        if not ends(b):
                            stages(u, first, last, (0, lambda c: spread(spread_sems[1], n, c)))
                pipelined(act, BIT, sums)
            over_batches(act, batch)

        @block.tensor
        def _(pe):
            def transposes(sems, n, c):
                made, turned = sems[0:2]
                wait(pe, made, n[c + 1])
                for i in range(GROUP):
                    last_one = nc.tensor.transpose(k.psum[c % 2][:, i * P:(i + 1) * P], a_onehot[:, c, i, :], k.ident[:, :])
                last_one.then_inc(turned, 1)

            def expand(sems, n, step, column, c):
                copied, used = sems[2:4]
                at = load_offsets(k, pe, SPREAD_ROW, step + c * GROUP, GROUP, 2)
                wait(pe, copied, n[c + 1])
                for i in range(GROUP):
                    last_one = nc.tensor.matmul(k.psum[2][:, ds(column + (c * GROUP + i) * 2, 2)], k.onehot_t[:, c % 2, i, :],
                                                k.small[:, ds(at[i], 2)], start=True, stop=True)
                last_one.then_inc(used, 1)

            def spread_first(it, first, last):
                n = counts(pe, it * UNROLL, -1, 4)
                column = it * ITER * 2
                for u in range(UNROLL):
                    stages(u, first, last, (2, lambda c: expand(spread_sems[0], n, it * ITER, column, c)),
                           (0, lambda c: transposes(spread_sems[0], n, c)))
            pipelined(pe, BIT, spread_first)

            def batch(b, p, turn):
                first_group = b * BGROUPS
                pe.wait_ge(s_sc, b + 1)
                for j in range(3):
                    last = nc.tensor.transpose(k.psum[3][:, j * P:(j + 1) * P], x3[:, j, :], k.ident[:, :])
                last.then_inc(s_x3, 1)
                pe.wait_ge(s_cc, 2 * b + 2)
                for j in range(4):
                    last = nc.tensor.transpose(k.psum[4][0:1, j * P:(j + 1) * P], cols[:, j:j + 1], k.ident[:, :])
                last.then_inc(s_cr, 1)
                pe.wait_ge(s_tu, 2 * b + 2)
                nc.tensor.matmul(k.psum[5][:, 0:1], t_row[:, 0:P], k.ones_row[:, 0:1], start=True, stop=True)
                nc.tensor.matmul(k.psum[5][:, 1:2], u_row[:, 1:P + 1], k.ones_row[:, 0:1], start=True, stop=True).then_inc(s_tub, 1)
                pe.wait_ge(s_fb, 2 * b + 2)
                nc.tensor.matmul(k.psum[5][:, 8:10], k.ones_row[:, :], fpair, start=True, stop=True).then_inc(s_fv, 1)
                pe.wait_ge(s_w, b + 1)
                for j in range(2):
                    last = nc.tensor.transpose(k.psum[3][:, j * P:(j + 1) * P], wx[:, j, :], k.ident[:, :])
                last.then_inc(s_wt, 1)

                def sums(it, first, last):
                    n = counts(pe, first_group + it * UNROLL, -1, 4)
                    column = it * ITER * 2 if isinstance(it, int) else pe.snap(it * (ITER * 2))

                    def segment_sum(c):
                        wait(pe, e_m, n[c + 1])
                        wait(pe, e_S, n[c + 1])
                        wait(pe, e_acc, n[c])
                        for i in range(GROUP):
                            last_one = nc.tensor.matmul(k.psum[6 + c % 2][:, i * P:i * P + C + 2], k.onehot[:, c % UNROLL, i, :],
                                                        k.msg[:, c % UNROLL, i, 0:C + 2], start=True, stop=True)
                        last_one.then_inc(e_agg, 1)
                    for u in range(UNROLL):
                        stages(u, first, last, (1, segment_sum))
                        if not ends(b):
                            stages(u, first, last, (2, lambda c: expand(spread_sems[1], n, (b * BIT + it) * ITER + P, column, c)),
                                   (0, lambda c: transposes(spread_sems[1], n, c)))
                pipelined(pe, BIT, sums)
            over_batches(pe, batch)


def gat_finish(k, layer, out):
    nc = k.nc
    k.next_stage()
    n = f"gat{layer}_f_"
    s_ch, s_in, s_aout, s_mm, s_x, s_st = (k.sem(n + x) for x in ("chain", "act_in", "act_out", "colsum", "x1", "store"))
    sq = k.big[:, 0:NB * C].rearrange("p (b c) -> p b c", c=C)
    selfw, den = k.node_col[:, 0, :], k.node_col[:, 1, :]
    psums = k.work[:, 0:C]
    mean = k.work[:, C:2 * C]
    std = k.work[:, 2 * C:3 * C]
    bias, gamma, beta = (k.gvec[:, 3 * layer + j, :] for j in range(3))
    a = k.node_a

    def over_nodes(vec):
        return vec.unsqueeze(1).broadcast_to([P, NB, C])

    def over_chan(vec):
        return vec.unsqueeze(2).broadcast_to([P, NB, C])

    with nc.Block() as block:
        @block.vector
        def _(v):
            link = Chain(v, s_ch)
            link(nc.vector.tensor_scalar(selfw, k.loop_sum[:, :, 2], 0.0, None, ALU.is_equal))
            link(nc.vector.tensor_tensor(selfw, selfw, k.acc[:, :, C + 1], ALU.add))
            link(nc.vector.tensor_tensor(den, selfw, k.acc[:, :, C], ALU.add))
            link(nc.vector.reciprocal(den, den))
            link(nc.vector.tensor_tensor(a, k.node_b, over_chan(selfw), ALU.mult))
            link(nc.vector.tensor_tensor(a, a, k.acc[:, :, 0:C], ALU.add))
            link(nc.vector.tensor_tensor(a, a, over_chan(den), ALU.mult))
            link(nc.vector.tensor_tensor(a, a, over_nodes(bias), ALU.add))
            link(nc.vector.tensor_scalar(a[:, NB - 1, :], a[:, NB - 1, :], k.row_mask[:, :], None, ALU.mult))
            nc.vector.tensor_reduce(psums, a.rearrange("p b c -> p c b"), AX.X, ALU.add).then_inc(s_in, 1)
            v.wait_ge(s_mm, 1)
            link(nc.vector.tensor_scalar(mean, k.psum[0][:, 0:C], 1.0 / N, None, ALU.mult))
            link(nc.vector.tensor_tensor(a, a, over_nodes(mean), ALU.subtract))
            nc.vector.tensor_scalar(a[:, NB - 1, :], a[:, NB - 1, :], k.row_mask[:, :], None, ALU.mult).then_inc(s_in, 1)
            v.wait_ge(s_aout, 1)
            nc.vector.tensor_reduce(psums, sq.rearrange("p b c -> p c b"), AX.X, ALU.add).then_inc(s_in, 1)
            v.wait_ge(s_mm, 2)
            nc.vector.tensor_scalar(std, k.psum[0][:, C:2 * C], 1.0 / N, EPS, ALU.mult, ALU.add).then_inc(s_in, 1)
            v.wait_ge(s_aout, 2)
            link(nc.vector.reciprocal(std, std))
            link(nc.vector.tensor_tensor(std, std, gamma, ALU.mult))
            link(nc.vector.tensor_tensor(a, a, over_nodes(std), ALU.mult))
            link(nc.vector.tensor_tensor(a, a, over_nodes(beta), ALU.add))
            if layer == 0:
                link(nc.vector.tensor_scalar(a, a, 0.0, None, ALU.max))
                return
            v.wait_ge(s_x, 16)
            link(nc.vector.tensor_tensor(a, a, k.node_b, ALU.add))
            layer_norm(nc, k, v, link, sq, s_in, s_aout, 2)

        @block.tensor
        def _(pe):
            pe.wait_ge(s_in, 1)
            nc.tensor.matmul(k.psum[0][:, 0:C], k.ones_sq[:, :], psums, start=True, stop=True).then_inc(s_mm, 1)
            pe.wait_ge(s_in, 3)
            nc.tensor.matmul(k.psum[0][:, C:2 * C], k.ones_sq[:, :], psums, start=True, stop=True).then_inc(s_mm, 1)

        @block.scalar
        def _(act):
            act.wait_ge(s_in, 2)
            nc.scalar.activation(sq, a, ACT.Square).then_inc(s_aout, 1)
            act.wait_ge(s_in, 4)
            nc.scalar.activation(std, std, ACT.Sqrt).then_inc(s_aout, 1)
            if layer == 1:
                layer_norm_act(nc, k, act, sq, s_in, s_aout, 4)

        @block.sync
        def _(sp):
            k.clear_old(sp)
            if layer == 1:
                sp.wait_ge(s_ch, 5)
                sp.dma_start(k.node_b, k.x1_dram.rearrange("(b p) c -> p b c", p=P)).then_inc(s_x, 16)
                sp.wait_ge(s_ch, GAT_LINKS)
                full = (NB - 1) * P
                sp.dma_start(out[0:full, :].rearrange("(b p) c -> p b c", p=P), k.node_a[:, 0:NB - 1, :]).then_inc(s_st, 16)
                sp.dma_start(out[full:N, :], k.node_a[0:LAST, NB - 1, :]).then_inc(s_st, 16)
                sp.wait_ge(s_st, 32)


GAT_LINKS = 21


def gnn_resnorm_kernel(nc, a, out, upto=99):
    ctx = ExitStack()
    with ctx:
        k = Core(nc, ctx)
        setup(k, a)
        for layer in range(2):
            cg_tables(k, layer)
            cg_edges(k, layer)
            cg_finish(k, layer, a["x"])
        for layer in range(2):
            gat_tables(k, layer)
            gat_edges(k, layer)
            gat_finish(k, layer, out)
        k.close()


_INS = ["x", "src", "dst", "edge_attr_16",
        "L0_gnn_Wf1", "L0_gnn_bf1", "L0_gnn_Ws1", "L0_gnn_bs1", "L0_gnn_Wf2", "L0_gnn_bf2", "L0_gnn_Ws2", "L0_gnn_bs2",
        "L1_gnn_W0", "L1_gnn_We0", "L1_gnn_as0", "L1_gnn_ad0", "L1_gnn_ae0", "L1_gnn_b0", "L1_gnn_g0", "L1_gnn_beta0",
        "L1_gnn_W1", "L1_gnn_We1", "L1_gnn_as1", "L1_gnn_ad1", "L1_gnn_ae1", "L1_gnn_b1", "L1_gnn_gf", "L1_gnn_betaf"]


def kernel(**inputs):
    import numpy as np
    import concourse.bacc as bacc
    from concourse.bass_utils import run_bass_kernel_spmd as run

    nc = bacc.Bacc("TRN2", target_bir_lowering=False, num_devices=1)
    arrays, aps = {}, {}
    for name in _INS:
        arr = np.ascontiguousarray(inputs[name])
        arrays["in_" + name] = arr
        aps[name] = nc.dram_tensor("in_" + name, arr.shape, mybir.dt.from_np(arr.dtype), kind="ExternalInput").ap()
    out = nc.dram_tensor("out_0", (N, C), F32, kind="ExternalOutput").ap()
    gnn_resnorm_kernel(nc, aps, out)
    r = run(nc, [arrays], core_ids=[0])
    return r.results[0]["out_0"]
```
